# Optimizing a Trainium2 kernel written in Bass

```python
import numpy as np
import jax
import jax.numpy as jnp

def _softmax(x, axis=-1):
    return jax.nn.softmax(x, axis=axis)

def _gelu(x):
    return jax.nn.gelu(x, approximate=True)

def _silu(x):
    return jax.nn.silu(x)

def _sigmoid(x):
    return jax.nn.sigmoid(x)

def _layernorm(x, axis=-1, eps=1e-05):
    m = jnp.mean(x, axis=axis, keepdims=True)
    v = jnp.var(x, axis=axis, keepdims=True)
    return (x - m) / jnp.sqrt(v + eps)

def _scatter_add(tgt, idx, src, axis=0):
    return tgt.at[idx].add(src)

def _segment_sum(src, seg, n):
    return jax.ops.segment_sum(src, seg, n)
kernel_name = 'mk_macaron_d1_jaxref_r4_82e7c3'

def setup_inputs(seed: int=0):
    np.random.seed(seed)
    _w = jnp.asarray

    def _L0_attn_setup():
        import jax, jax.numpy as jnp
        import numpy as np
        B, L, E, H = (1, 1024, 256, 16)
        D = E // H
        EPS = 1e-06
        key = jax.random.key(seed)
        k1, k2, k3 = jax.random.split(key, 3)
        x = jax.random.normal(k1, (B, L, E), dtype=jnp.float32)
        qkv_w = jax.random.normal(k2, (E, 3 * E), dtype=jnp.float32) / np.sqrt(E)
        qkv_b = jnp.zeros((3 * E,), dtype=jnp.float32)
        out_w = jax.random.normal(k3, (E, E), dtype=jnp.float32) / np.sqrt(E)
        out_b = jnp.zeros((E,), dtype=jnp.float32)
        return {'x': x, 'qkv_w': qkv_w, 'qkv_b': qkv_b, 'out_w': out_w, 'out_b': out_b}
    _L0_attn_in = _L0_attn_setup()

    def _L0_ffn_setup():
        import jax, jax.numpy as jnp
        import numpy as np
        DIM = 256
        HIDDEN = 768
        SCALE = 1.0 / 127.0

        def _dequant(w_int, dtype):
            return w_int.astype(dtype) * jnp.asarray(SCALE, dtype)
        key = jax.random.key(seed)
        k_x, k_g, k_u, k_d = jax.random.split(key, 4)
        x = jax.random.normal(k_x, (4, 512, DIM), dtype=jnp.float32)
        w_gate = jax.random.randint(k_g, (HIDDEN, DIM), -127, 128, dtype=jnp.int32)
        w_up = jax.random.randint(k_u, (HIDDEN, DIM), -127, 128, dtype=jnp.int32)
        w_down = jax.random.randint(k_d, (DIM, HIDDEN), -127, 128, dtype=jnp.int32)
        return {'x': x, 'w_gate': w_gate, 'w_up': w_up, 'w_down': w_down}
    _L0_ffn_in = _L0_ffn_setup()
    _d = {'L0_attn_x': _L0_attn_in['x'], 'L0_attn_qkv_w': _L0_attn_in['qkv_w'], 'L0_attn_qkv_b': _L0_attn_in['qkv_b'], 'L0_attn_out_w': _L0_attn_in['out_w'], 'L0_attn_out_b': _L0_attn_in['out_b'], 'L0_ffn_w_gate': _L0_ffn_in['w_gate'], 'L0_ffn_w_up': _L0_ffn_in['w_up'], 'L0_ffn_w_down': _L0_ffn_in['w_down']}
    _x0 = _d['L0_attn_x']
    _d['L0_attn_x'] = jax.random.normal(jax.random.fold_in(jax.random.key(seed), 1), (8, 1024, 256), dtype=_x0.dtype)
    del _x0
    return _d

def reference(L0_attn_x, L0_attn_qkv_w, L0_attn_qkv_b, L0_attn_out_w, L0_attn_out_b, L0_ffn_w_gate, L0_ffn_w_up, L0_ffn_w_down):

    def _L0_attn_ref(x, qkv_w, qkv_b, out_w, out_b):
        import jax, jax.numpy as jnp
        import numpy as np
        B, L, E, H = (1, 1024, 256, 16)
        D = E // H
        EPS = 1e-06
        b, l, e = x.shape
        qkv = x @ qkv_w + qkv_b
        q, k, v = jnp.split(qkv, 3, axis=-1)
        q = q.reshape(b, l, H, D).transpose(0, 2, 1, 3)
        k = k.reshape(b, l, H, D).transpose(0, 2, 1, 3)
        v = v.reshape(b, l, H, D).transpose(0, 2, 1, 3)
        q_prime = jax.nn.elu(q) + 1.0
        k_prime = jax.nn.elu(k) + 1.0
        kv_prod = jnp.einsum('bhld,bhle->bhlde', k_prime, v)
        kv_cumsum = jnp.cumsum(kv_prod, axis=2)
        context = jnp.einsum('bhld,bhlde->bhle', q_prime, kv_cumsum)
        k_cumsum = jnp.cumsum(k_prime, axis=2)
        norm = jnp.einsum('bhld,bhld->bhl', q_prime, k_cumsum)
        output = context / (norm[..., None] + EPS)
        output = output.transpose(0, 2, 1, 3).reshape(b, l, e)
        return output @ out_w + out_b

    def _L0_ffn_ref(x, w_gate, w_up, w_down):
        import jax, jax.numpy as jnp
        import numpy as np
        DIM = 256
        HIDDEN = 768
        SCALE = 1.0 / 127.0

        def _dequant(w_int, dtype):
            return w_int.astype(dtype) * jnp.asarray(SCALE, dtype)
        wg = _dequant(w_gate, x.dtype)
        wu = _dequant(w_up, x.dtype)
        wd = _dequant(w_down, x.dtype)
        gate = jnp.einsum('bsd,hd->bsh', x, wg)
        up = jnp.einsum('bsd,hd->bsh', x, wu)
        h = jax.nn.silu(gate) * up
        return jnp.einsum('bsh,dh->bsd', h, wd)
    x = L0_attn_x
    x = x + 0.5 * _L0_ffn_ref(_layernorm(x, axis=-1), L0_ffn_w_gate, L0_ffn_w_up, L0_ffn_w_down)
    x = x + _L0_attn_ref(_layernorm(x, axis=-1), L0_attn_qkv_w, L0_attn_qkv_b, L0_attn_out_w, L0_attn_out_b)
    x = x + 0.5 * _L0_ffn_ref(_layernorm(x, axis=-1), L0_ffn_w_gate, L0_ffn_w_up, L0_ffn_w_down)
    return x

_drawn_inputs = setup_inputs


def setup_inputs(seed=0):
    import zlib

    import numpy as np

    out = dict(_drawn_inputs(seed))
    spreads = {'L0_attn_qkv_b': (0.0, 2.0), 'L0_attn_out_b': (0.0, 2.0)}
    factors = {'L0_attn_qkv_w': 24.792, 'L0_attn_out_w': 8.0}
    for name, (base, spread) in spreads.items():
        noise = np.random.default_rng([zlib.crc32(name.encode()), seed]).standard_normal(out[name].shape)
        drawn = base * np.exp(spread * noise) if base else spread * noise
        out[name] = jnp.asarray(drawn.astype(out[name].dtype))
    for name, factor in factors.items():
        out[name] = (out[name] * factor).astype(out[name].dtype)
    return out
```

```python
from contextlib import ExitStack

import concourse.bass as bass
from concourse import mybir

FP32 = mybir.dt.float32
FP16 = mybir.dt.float16
I32 = mybir.dt.int32
ALU = mybir.AluOpType
ACT = mybir.ActivationFunctionType
AX = mybir.AxisListType

P = 128
B, L, E, H = 8, 1024, 256, 16
D = E // H
F = 768
HALF = L // 2
T = HALF // P
KE = E // P
KF = F // P
LN_EPS = 1e-5
DEN_EPS = 1e-6
W_SCALE = 1.0 / 127.0

BIG = 0
TR = 4
DOWN = 6
NUM = 6
STATE = 7

N_LN = 6
N_GU = 4 * KF
N_DN = 8
N_CH = 2 * T
N_PROJ = 8
N_VP = 4


def build(nc, x, w_gate, w_up, w_down, w_qkv, b_cols, b_v, w_out, b_out, out):
    x_t = x.rearrange("b (h t p) e -> b h p t e", h=2, p=P)
    out_t = out.rearrange("b (h t p) e -> b h p t e", h=2, p=P)

    with ExitStack() as ctx:
        def sb(name, shape, dt=FP32):
            return ctx.enter_context(nc.sbuf_tensor(name, shape, dt))

        def sem(name):
            return ctx.enter_context(nc.semaphore(name))

        ps = ctx.enter_context(nc.psum_tensor("ps", [P, 8, 512], FP32))

        wg = sb("wg", [P, KE, F])
        wu = sb("wu", [P, KE, F])
        wd = sb("wd", [P, KF, E])
        wqkv = sb("wqkv", [P, KE, 3 * E])
        wo = sb("wo", [P, KE, E])
        bqk = sb("bqk", [P, 4])
        minus_bqk = sb("minus_bqk", [P, 4])
        bv_row = sb("bv_row", [1, E])
        bo_row = sb("bo_row", [1, E])
        bv = sb("bv", [P, E])
        bo = sb("bo", [P, E])
        ident = sb("ident", [P, P])
        causal = sb("causal", [P, P])
        same_head = sb("same_head", [P, P])
        parity = sb("parity", [P, 2])
        ones = sb("ones", [P, HALF])
        minus_half = sb("minus_half", [P, T])
        den_eps = sb("den_eps", [P, 1])
        xin = sb("xin", [P, 2, T, E])
        xr = sb("xr", [P, 2, T, E])
        xb = sb("xb", [P, 2, T, E])
        xn = sb("xn", [P, 2, T, E])
        xT = sb("xT", [P, 2, KE, HALF])
        stats = sb("stats", [P, T, 6])
        mean2 = sb("mean2", [P, T])
        gap = sb("gap", [P, T])
        gap2 = sb("gap2", [P, T])
        dev = sb("dev", [P, T])
        mean = sb("mean", [P, T])
        var_eps = sb("var_eps", [P, T])
        rstd = sb("rstd", [P, T])
        silu = sb("silu", [P, 2, HALF])
        hT = sb("hT", [P, 2, KF, HALF])
        elu_m = sb("elu_m", [P, 2, HALF])
        elu_e = sb("elu_e", [P, 2, HALF])
        elu_r = sb("elu_r", [P, 2, HALF])
        kT = sb("kT", [P, KE, HALF])
        qT = sb("qT", [P, KE, HALF])
        qz = sb("qz", [P, KE, 2, HALF])
        kcum = sb("kcum", [P, 2, KE, HALF])
        z = sb("z", [P, KE, HALF])
        k_tok = sb("k_tok", [P, T, E])
        v_tok = sb("v_tok", [P, T, H, 2 * D])
        scores = sb("scores", [P, 4, KE, 2, P])
        state = sb("state", [P, KE, P])
        den = sb("den", [P, KE, HALF])
        rden = sb("rden", [P, KE, HALF])
        oT = sb("oT", [P, KE, HALF])

        w_loaded = sem("w_loaded")
        consts_ready = sem("consts_ready")
        setup_steps = sem("setup_steps")
        bias_rows_done = sem("bias_rows_done")
        weights_ready = sem("weights_ready")
        x_loaded = [sem("x_loaded_a"), sem("x_loaded_b")]
        x_stored = [sem("x_stored_a"), sem("x_stored_b")]
        stats_done = sem("stats_done")
        sums_done = sem("sums_done")
        mean_done = sem("mean_done")
        var_ready = sem("var_ready")
        rstd_ready = sem("rstd_ready")
        xn_ready = sem("xn_ready")
        xt_done = sem("xt_done")
        xt_copied = sem("xt_copied")
        gu_done = sem("gu_done")
        silu_done = sem("silu_done")
        h_done = sem("h_done")
        dn_done = sem("dn_done")
        res_done = sem("res_done")
        xb_done = sem("xb_done")
        vp_done = sem("vp_done")
        v_done = sem("v_done")
        proj_done = sem("proj_done")
        relu_done = sem("relu_done")
        elu_done = sem("elu_done")
        kq_done = sem("kq_done")
        kt_done = sem("kt_done")
        ktok_done = sem("ktok_done")
        qz_done = sem("qz_done")
        kcum_done = sem("kcum_done")
        z_done = sem("z_done")
        den_done = sem("den_done")
        den_copied = sem("den_copied")
        rden_done = sem("rden_done")
        s_done = sem("s_done")
        masked = sem("masked")
        ku_done = sem("ku_done")
        state_done = sem("state_done")
        pv_done = sem("pv_done")
        o_done = sem("o_done")
        op_done = sem("op_done")
        res2_done = sem("res2_done")

        block = ctx.enter_context(nc.Block())

        def v_heads(t, f):
            return v_tok[:, t, f * 8:f * 8 + 8, 0:D]

        def v_padded(t, h):
            flat = v_tok[:, t].rearrange("p h d -> p (h d)")
            at = 2 * D * h - D * (h % 2)
            return flat[:, at:at + 2 * D]

        @block.sync
        def _(sp):
            for dst, src in ((wg, w_gate), (wu, w_up), (wd, w_down)):
                sp.dma_start(dst[:, :, :].bitcast(I32), src.rearrange("(k p) n -> p k n", p=P)).then_inc(w_loaded, 16)
            for h in range(2):
                sp.dma_start(xin[:, h], x_t[0, h]).then_inc(x_loaded[h], 16)
            for dst, src in ((wqkv, w_qkv), (wo, w_out)):
                sp.dma_start(dst[:, :, :], src.rearrange("(k p) n -> p k n", p=P)).then_inc(w_loaded, 16)
            sp.dma_start(bqk[:, :], b_cols).then_inc(w_loaded, 16)
            sp.dma_start(bv_row[:, :], b_v).then_inc(w_loaded, 16)
            sp.dma_start(bo_row[:, :], b_out).then_inc(w_loaded, 16)
            with sp.Fori(1, B) as b:
                for h in range(2):
                    sp.wait_ge(res_done, b * N_DN + (2 * h + 2 + 2 - N_DN))
                    sp.dma_start(xin[:, h], x_t[b, h]).then_inc(x_loaded[h], 16)
                for h in range(2):
                    sp.wait_ge(res_done, b * N_DN + (4 + 2 * h + 2 + 2 - N_DN))
                    sp.dma_start(out_t[b - 1, h], xr[:, h]).then_inc(x_stored[h], 16)
            for h in range(2):
                sp.wait_ge(res_done, (B - 1) * N_DN + 2 * h + 2 + 2)
                sp.dma_start(xin[:, h], x_t[B - 1, h]).then_inc(x_loaded[h], 16)
            for h in range(2):
                sp.wait_ge(res_done, (B - 1) * N_DN + 4 + 2 * h + 2 + 2)
                sp.dma_start(out_t[B - 1, h], xr[:, h]).then_inc(x_stored[h], 16)
            for h in range(2):
                sp.wait_ge(x_stored[h], 16 * (B + 1))

        @block.gpsimd
        def _(pool):
            nc.gpsimd.memset(ident[:, :], 0.0)
            nc.gpsimd.memset(causal[:, :], 1.0)
            nc.gpsimd.memset(same_head[:, :], 1.0)
            nc.gpsimd.memset(minus_half[:, :], -0.5)
            nc.gpsimd.memset(den_eps[:, :], DEN_EPS).then_inc(consts_ready, 1)
            pool.wait_ge(consts_ready, 1)
            nc.gpsimd.affine_select(out=ident[:, :], in_=ident[:, :], compare_op=ALU.not_equal, fill=1.0,
                                    base=0, pattern=[[-1, P]], channel_multiplier=1)
            nc.gpsimd.affine_select(out=causal[:, :], in_=causal[:, :], compare_op=ALU.is_ge, fill=0.0,
                                    base=0, pattern=[[1, P]], channel_multiplier=-1)
            heads = same_head[:, :].rearrange("p (h d) -> p h d", d=D)
            nc.gpsimd.affine_select(out=heads, in_=heads, compare_op=ALU.is_ge, fill=0.0,
                                    base=0, pattern=[[-D, P // D], [0, D]], channel_multiplier=1).then_inc(consts_ready, 1)
            pool.wait_ge(consts_ready, 2)
            nc.gpsimd.affine_select(out=heads, in_=heads, compare_op=ALU.is_ge, fill=0.0,
                                    base=D - 1, pattern=[[D, P // D], [0, D]], channel_multiplier=-1).then_inc(consts_ready, 1)

            def pow_rstd(at):
                pool.wait_ge(var_ready, at)
                nc.gpsimd.tensor_tensor(rstd[:, :], var_eps[:, :], minus_half[:, :], ALU.pow).then_inc(rstd_ready, 1)

            def add_b_out(b, h):
                pool.wait_ge(res_done, b * N_DN + (2 * h + 2 + 2))
                nc.gpsimd.tensor_tensor(xb[:, h], xr[:, h], bo[:, :].unsqueeze(1).broadcast_to([P, T, E]),
                                        ALU.add).then_inc(xb_done, 1)

            def spread_q(b, h):
                for f in range(KE):
                    pool.wait_ge(kq_done, b * N_PROJ + (4 * h + 2 + f + 1 + 2))
                    for v in range(2):
                        last = nc.gpsimd.tensor_tensor(qz[:, f, v, :], qT[:, f, :],
                                                       parity[:, v:v + 1].broadcast_to([P, HALF]), ALU.mult)
                    last.then_inc(qz_done, 1)
                for f in range(KE):
                    pool.wait_ge(kcum_done, b * 4 + (2 * h + f + 1))
                    nc.gpsimd.tensor_tensor(z[:, f, :], qT[:, f, :], kcum[:, h, f, :], ALU.mult).then_inc(z_done, 1)

            pool.wait_ge(weights_ready, 1)
            pow_rstd(1)
            pow_rstd(2)
            with pool.Fori(0, B) as b:
                ln = b * N_LN
                pow_rstd(ln + 3)
                add_b_out(b, 0)
                pow_rstd(ln + 4)
                add_b_out(b, 1)
                spread_q(b, 0)
                pow_rstd(ln + 5)
                spread_q(b, 1)
                pow_rstd(ln + 6)
                pow_rstd(ln + 7)
                pow_rstd(ln + 8)

        @block.scalar
        def _(act):
            c_gate = W_SCALE
            c_att = 1.0

            def copy_xt(at):
                act.wait_ge(xt_done, at)
                h = act_half[0]
                act_half[0] ^= 1
                nc.scalar.activation(xT[:, h], ps[:, TR:TR + KE, :], ACT.Copy).then_inc(xt_copied, 1)

            act_half = [0]

            def gate(b, ffn, h):
                for m in range(KF):
                    n = (2 * ffn + h) * KF + m
                    act.wait_ge(gu_done, b * N_GU + (n + 1))
                    act.wait_ge(h_done, b * N_GU + (n - 1 + 2))
                    nc.scalar.activation(silu[:, m % 2, :], ps[:, BIG + 2 * (m % 2), :], ACT.Silu,
                                         scale=c_gate).then_inc(silu_done, 1)

            def attention(b, h):
                for j in range(4):
                    bias = bqk[:, (2 + j) % 4:(2 + j) % 4 + 1]
                    minus_bias = minus_bqk[:, (2 + j) % 4:(2 + j) % 4 + 1]
                    act.wait_ge(proj_done, b * N_PROJ + (4 * h + j + 1))
                    act.wait_ge(kq_done, b * N_PROJ + (4 * h + j - 1 + 2))
                    nc.scalar.activation(elu_m[:, j % 2, :], ps[:, BIG + j, :], ACT.Relu, bias=minus_bias,
                                         scale=-c_att).then_inc(relu_done, 1)
                    nc.scalar.activation(elu_r[:, j % 2, :], ps[:, BIG + j, :], ACT.Relu, bias=bias, scale=c_att)
                    act.wait_ge(relu_done, b * N_PROJ + (4 * h + j + 1))
                    nc.scalar.activation(elu_e[:, j % 2, :], elu_m[:, j % 2, :], ACT.Exp,
                                         scale=-1.0).then_inc(elu_done, 1)
                for i in range(2):
                    act.wait_ge(kt_done, b * N_VP + (2 * h + i + 1))
                    nc.scalar.activation(k_tok[:, 2 * i:2 * i + 2, :],
                                         ps[:, TR + i, :].rearrange("p (t e) -> p t e", t=2),
                                         ACT.Copy).then_inc(ktok_done, 1)
                act.wait_ge(den_done, b * 2 + (h + 1))
                nc.scalar.activation(den[:, :, :], ps[:, TR:TR + KE, :], ACT.Identity,
                                     bias=den_eps[:, 0:1]).then_inc(den_copied, 1)

            act.wait_ge(consts_ready, 3)
            act.wait_ge(weights_ready, 1)
            copy_xt(1)
            copy_xt(2)
            with act.Fori(0, B) as b:
                ln = b * N_LN
                gate(b, 0, 0)
                gate(b, 0, 1)
                copy_xt(ln + 3)
                attention(b, 0)
                copy_xt(ln + 4)
                attention(b, 1)
                copy_xt(ln + 5)
                gate(b, 1, 0)
                copy_xt(ln + 6)
                gate(b, 1, 1)
                copy_xt(ln + 7)
                copy_xt(ln + 8)

        @block.vector
        def _(dve):
            c_up = W_SCALE
            c_down = 0.5 * W_SCALE
            c_att = 1.0
            c_op = 1.0

            nc.vector.memset(ones[:, :], 1.0)
            nc.vector.memset(state[:, :, :], 0.0).then_inc(state_done, 1)
            nc.vector.memset(v_tok[:, :, :, :], 0.0).then_inc(setup_steps, 1)
            dve.wait_ge(w_loaded, 16 * 8)
            for w in (wg, wu):
                nc.vector.tensor_copy(w[:, :, :], w[:, :, :].bitcast(I32)).then_inc(h_done, 1)
            nc.vector.tensor_copy(wd[:, 0:3], wd[:, 0:3].bitcast(I32)).then_inc(res_done, 1)
            nc.vector.tensor_copy(wd[:, 3:6], wd[:, 3:6].bitcast(I32)).then_inc(res_done, 1)
            nc.vector.tensor_scalar(minus_bqk[:, :], bqk[:, :], -1.0, None, ALU.mult)
            dve.wait_ge(consts_ready, 3)
            for v in range(2):
                nc.vector.tensor_reduce(parity[:, v:v + 1], same_head[:, v * D:P:2 * D], AX.X, ALU.add).then_inc(kq_done, 1)
            dve.wait_ge(bias_rows_done, 1)
            nc.vector.tensor_copy(bv[:, :], ps[:, TR, 0:E])
            nc.vector.tensor_copy(bo[:, :], ps[:, TR, E:2 * E]).then_inc(weights_ready, 1)

            def ln_stats(src, at, load=None):
                if load is not None:
                    dve.wait_ge(*load)
                for t in range(T):
                    last = nc.vector.bn_stats(stats[:, t, :], src[:, t, :])
                last.then_inc(stats_done, 1)
                dve.wait_ge(stats_done, at)
                mean_e, dev_e, mean_o, dev_o = (stats[:, :, i] for i in (1, 2, 4, 5))
                nc.vector.tensor_tensor(mean2[:, :], mean_e, mean_o, ALU.add)
                nc.vector.tensor_tensor(gap[:, :], mean_e, mean_o, ALU.subtract)
                nc.vector.scalar_tensor_tensor(out=dev[:, :], in0=dev_e, scalar=E * LN_EPS, in1=dev_o,
                                               op0=ALU.add, op1=ALU.add).then_inc(sums_done, 1)
                dve.wait_ge(sums_done, at)
                nc.vector.tensor_scalar(mean[:, :], mean2[:, :], 0.5, None, ALU.mult)
                nc.vector.scalar_tensor_tensor(out=gap2[:, :], in0=gap[:, :], scalar=0.25, in1=gap[:, :],
                                               op0=ALU.mult, op1=ALU.mult).then_inc(mean_done, 1)
                dve.wait_ge(mean_done, at)
                nc.vector.scalar_tensor_tensor(out=var_eps[:, :], in0=dev[:, :], scalar=1.0 / E, in1=gap2[:, :],
                                               op0=ALU.mult, op1=ALU.add).then_inc(var_ready, 1)

            def ln_apply(src, h, at):
                dve.wait_ge(rstd_ready, at)
                dve.wait_ge(xt_done, at - 2)
                for t in range(T):
                    last = nc.vector.tensor_scalar(xn[:, h, t, :], src[:, t, :], mean[:, t:t + 1],
                                                   rstd[:, t:t + 1], ALU.subtract, ALU.mult)
                last.then_inc(xn_ready, 1)

            def gate_times_up(b, ffn, h, tiles=range(KF)):
                for m in tiles:
                    n = (2 * ffn + h) * KF + m
                    dve.wait_ge(silu_done, b * N_GU + (n + 1))
                    nc.vector.scalar_tensor_tensor(out=hT[:, h, m, :], in0=ps[:, BIG + 2 * (m % 2) + 1, :],
                                                   scalar=c_up, in1=silu[:, m % 2, :],
                                                   op0=ALU.mult, op1=ALU.mult).then_inc(h_done, 1)

            def residual(b, ffn, h):
                if ffn == 0:
                    dve.wait_ge(x_stored[h], b * 16 + 16)
                for i in range(2):
                    src = (xr if ffn else xin)[:, h, 2 * i:2 * i + 2, :]
                    dve.wait_ge(dn_done, b * N_DN + (4 * ffn + 2 * h + i + 1))
                    nc.vector.scalar_tensor_tensor(out=xr[:, h, 2 * i:2 * i + 2, :],
                                                   in0=ps[:, DOWN + i, :].rearrange("p (t e) -> p t e", t=2),
                                                   scalar=c_down, in1=src,
                                                   op0=ALU.mult, op1=ALU.add).then_inc(res_done, 1)

            def attention_in(b, h):
                for i in range(2):
                    dve.wait_ge(vp_done, b * N_VP + (2 * h + i + 1))
                    for t in (2 * i, 2 * i + 1):
                        last = nc.vector.scalar_tensor_tensor(
                            out=v_tok[:, t, :, 0:D],
                            in0=ps[:, TR + i, (t % 2) * E:(t % 2) * E + E].rearrange("p (h d) -> p h d", d=D),
                            scalar=c_att, in1=bv[:, :].rearrange("p (h d) -> p h d", d=D),
                            op0=ALU.mult, op1=ALU.add)
                    last.then_inc(v_done, 1)
                for j in range(4):
                    dst = (kT, qT)[j // 2][:, j % 2, :]
                    dve.wait_ge(elu_done, b * N_PROJ + (4 * h + j + 1))
                    nc.vector.tensor_tensor(dst, elu_e[:, j % 2, :], elu_r[:, j % 2, :], ALU.add).then_inc(kq_done, 1)
                for f in range(KE):
                    dve.wait_ge(kq_done, b * N_PROJ + (4 * h + f + 1 + 2))
                    if h:
                        dve.wait_ge(kcum_done, b * 4 + (f + 1))
                    nc.vector.tensor_tensor_scan(kcum[:, h, f, :], ones[:, :], kT[:, f, :],
                                                 kcum[:, 0, f, HALF - 1:HALF] if h else 0.0,
                                                 ALU.mult, ALU.add).then_inc(kcum_done, 1)

            def attention_chunks(b, h):
                for c in range(T):
                    n = T * h + c
                    for i in range(2):
                        dve.wait_ge(s_done, b * 2 * N_CH + (2 * n + i + 1))
                        nc.vector.tensor_tensor(
                            scores[:, 2 * i:2 * i + 2].rearrange("p g f v q -> p (g f v) q"),
                            ps[:, BIG + 2 * i:BIG + 2 * i + 2, :].rearrange("p g (x q) -> p (g x) q", q=P),
                            causal[:, :].unsqueeze(1).broadcast_to([P, 8, P]), ALU.mult).then_inc(masked, 1)
                    if n < N_CH - 1:
                        dve.wait_ge(ku_done, b * (N_CH - 1) + (n + 1))
                        nc.vector.tensor_tensor(state[:, :, :],
                                                ps[:, STATE, 0:KE * P].rearrange("p (f e) -> p f e", f=KE),
                                                same_head[:, :].unsqueeze(1).broadcast_to([P, KE, P]),
                                                ALU.mult).then_inc(state_done, 1)
                    if c == 0:
                        dve.wait_ge(den_copied, b * 2 + (h + 1))
                        nc.vector.reciprocal(rden[:, :, :], den[:, :, :]).then_inc(rden_done, 1)
                        dve.wait_ge(rden_done, b * 2 + (h + 1))
                    dve.wait_ge(pv_done, b * N_CH + (n + 1))
                    nc.vector.tensor_tensor(oT[:, :, c * P:c * P + P],
                                            ps[:, NUM, 0:KE * P].rearrange("p (f q) -> p f q", f=KE),
                                            rden[:, :, c * P:c * P + P], ALU.mult).then_inc(o_done, 1)
                if h:
                    nc.vector.memset(state[:, :, :], 0.0).then_inc(state_done, 1)

            def attention_residual(b, h):
                dve.wait_ge(xb_done, b * 2 + (h + 1))
                for i in range(2):
                    dve.wait_ge(op_done, b * N_VP + (2 * h + i + 1))
                    nc.vector.scalar_tensor_tensor(out=xr[:, h, 2 * i:2 * i + 2, :],
                                                   in0=ps[:, TR + i, :].rearrange("p (t e) -> p t e", t=2),
                                                   scalar=c_op, in1=xb[:, h, 2 * i:2 * i + 2, :],
                                                   op0=ALU.mult, op1=ALU.add).then_inc(res2_done, 1)

            def own_residual(b, ffn, h):
                dve.wait_ge(res_done, b * N_DN + (4 * ffn + 2 * h + 2 + 2))

            ln_stats(xin[:, 0], 1, (x_loaded[0], 16))
            dve.wait_ge(rstd_ready, 1)
            for h in range(2):
                if h:
                    ln_stats(xin[:, 1], 2, (x_loaded[1], 16))
                    dve.wait_ge(rstd_ready, 2)
                for t in range(T):
                    last = nc.vector.tensor_scalar(xn[:, h, t, :], xin[:, h, t, :], mean[:, t:t + 1],
                                                   rstd[:, t:t + 1], ALU.subtract, ALU.mult)
                last.then_inc(xn_ready, 1)
            nc.vector.memset(xb[:, 0, 0, 0:1], 0.0).then_inc(x_stored[0], 16)
            nc.vector.memset(xb[:, 1, 0, 0:1], 0.0).then_inc(x_stored[1], 16)
            with dve.Fori(0, B) as b:
                ln = b * N_LN
                gate_times_up(b, 0, 0)
                gate_times_up(b, 0, 1)
                residual(b, 0, 0)
                own_residual(b, 0, 0)
                ln_stats(xr[:, 0], ln + 3)
                ln_apply(xr[:, 0], 0, ln + 3)
                residual(b, 0, 1)
                own_residual(b, 0, 1)
                ln_stats(xr[:, 1], ln + 4)
                attention_in(b, 0)
                ln_apply(xr[:, 1], 1, ln + 4)
                attention_chunks(b, 0)
                attention_residual(b, 0)
                dve.wait_ge(res2_done, b * 4 + 2)
                ln_stats(xr[:, 0], ln + 5)
                attention_in(b, 1)
                ln_apply(xr[:, 0], 0, ln + 5)
                attention_chunks(b, 1)
                attention_residual(b, 1)
                dve.wait_ge(res2_done, b * 4 + 4)
                ln_stats(xr[:, 1], ln + 6)
                gate_times_up(b, 1, 0, range(2))
                ln_apply(xr[:, 1], 1, ln + 6)
                gate_times_up(b, 1, 0, range(2, KF))
                ln_stats(xin[:, 0], ln + 7, (x_loaded[0], b * 16 + 32))
                gate_times_up(b, 1, 1, range(2))
                ln_apply(xin[:, 0], 0, ln + 7)
                ln_stats(xin[:, 1], ln + 8, (x_loaded[1], b * 16 + 32))
                gate_times_up(b, 1, 1, range(2, KF))
                ln_apply(xin[:, 1], 1, ln + 8)
                residual(b, 1, 0)
                residual(b, 1, 1)

        @block.tensor
        def _(pe):
            def transpose_xn(h, at):
                pe.wait_ge(xn_ready, at)
                for f in range(KE):
                    for t in range(T):
                        last = nc.tensor.transpose(ps[:, TR + f, t * P:t * P + P],
                                                   xn[:, h, t, f * P:f * P + P], ident[:, :])
                last.then_inc(xt_done, 1)

            def gate_up(b, ffn, h):
                for m in range(KF):
                    n = (2 * ffn + h) * KF + m
                    pe.wait_ge(h_done, b * N_GU + (n - 1 + 2))
                    for j, w in enumerate((wg, wu)):
                        for k in range(KE):
                            last = nc.tensor.matmul(ps[:, BIG + 2 * (m % 2) + j, :], w[:, k, m * P:m * P + P],
                                                    xT[:, h, k, :], start=(k == 0), stop=(k == KE - 1))
                    last.then_inc(gu_done, 1)

            def down(b, ffn, h):
                pe.wait_ge(h_done, b * N_GU + ((2 * ffn + h + 1) * KF + 2))
                for i in range(2):
                    pe.wait_ge(res_done, b * N_DN + (4 * ffn + 2 * h + i - 1 + 2))
                    for t in (2 * i, 2 * i + 1):
                        for k in range(KF):
                            last = nc.tensor.matmul(ps[:, DOWN + i, (t % 2) * E:(t % 2) * E + E],
                                                    hT[:, h, k, t * P:t * P + P], wd[:, k, :],
                                                    start=(k == 0), stop=(k == KF - 1))
                    last.then_inc(dn_done, 1)

            def attention(b, h):
                for i in range(2):
                    for t in (2 * i, 2 * i + 1):
                        for k in range(KE):
                            last = nc.tensor.matmul(ps[:, TR + i, (t % 2) * E:(t % 2) * E + E],
                                                    xT[:, h, k, t * P:t * P + P], wqkv[:, k, 2 * E:3 * E],
                                                    start=(k == 0), stop=(k == KE - 1))
                    last.then_inc(vp_done, 1)
                for j in range(4):
                    col = ((1, 1, 0, 0)[j]) * E + (j % 2) * P
                    for k in range(KE):
                        last = nc.tensor.matmul(ps[:, BIG + j, :], wqkv[:, k, col:col + P], xT[:, h, k, :],
                                                start=(k == 0), stop=(k == KE - 1))
                    last.then_inc(proj_done, 1)
                pe.wait_ge(kq_done, b * N_PROJ + (4 * h + 2 + 2))
                for i in range(2):
                    pe.wait_ge(v_done, b * N_VP + (2 * h + i + 1))
                    for t in (2 * i, 2 * i + 1):
                        for f in range(KE):
                            last = nc.tensor.transpose(ps[:, TR + i, (t % 2) * E + f * P:(t % 2) * E + f * P + P],
                                                       kT[:, f, t * P:t * P + P], ident[:, :])
                    last.then_inc(kt_done, 1)
                pe.wait_ge(qz_done, b * 4 + (2 * h + 2))
                for c in range(T):
                    n = T * h + c
                    tok = slice(c * P, c * P + P)
                    for i in range(2):
                        for g in (2 * i, 2 * i + 1):
                            rows = slice(32 * g, 32 * g + 32)
                            for f in range(KE):
                                last = nc.tensor.matmul(ps[:, BIG + g, f * 2 * P:(f + 1) * 2 * P],
                                                        kT[rows, f, tok], qz[rows, f, :, tok],
                                                        start=True, stop=True)
                        last.then_inc(s_done, 1)
                    pe.wait_ge(state_done, b * N_CH + (n + 1))
                    for f in range(KE):
                        nc.tensor.matmul(ps[:, NUM, f * P:f * P + P], state[:, f, :], qT[:, f, tok],
                                         start=(f == 0), stop=False, skip_group_check=True)
                    if c == 0:
                        pe.wait_ge(ktok_done, b * N_VP + (2 * h + 2))
                    if n < N_CH - 1:
                        for f in range(KE):
                            last = nc.tensor.matmul(ps[:, STATE, f * P:f * P + P], k_tok[:, c, f * P:f * P + P],
                                                    v_heads(c, f), start=(n == 0 and f == 0), stop=True,
                                                    skip_group_check=True)
                        last.then_inc(ku_done, 1)
                    if c == 0:
                        pe.wait_ge(z_done, b * 4 + (2 * h + 2))
                        for f in range(KE):
                            last = nc.tensor.matmul(ps[:, TR + f, :], same_head[:, :], z[:, f, :],
                                                    start=True, stop=True)
                        last.then_inc(den_done, 1)
                    for i in range(2):
                        pe.wait_ge(masked, b * 2 * N_CH + (2 * n + i + 1))
                        for g in (2 * i, 2 * i + 1):
                            for f in range(KE):
                                for v in range(2):
                                    last = nc.tensor.matmul(ps[32 * g:32 * g + 32, NUM, f * P:f * P + P],
                                                            v_padded(c, 8 * f + 2 * g + v),
                                                            scores[:, g, f, v, :], start=False, stop=True,
                                                            skip_group_check=True)
                    last.then_inc(pv_done, 1)
                    pe.wait_ge(o_done, b * N_CH + (n + 1))
                for i in range(2):
                    for t in (2 * i, 2 * i + 1):
                        for f in range(KE):
                            last = nc.tensor.matmul(ps[:, TR + i, (t % 2) * E:(t % 2) * E + E],
                                                    oT[:, f, t * P:t * P + P], wo[:, f, :],
                                                    start=(f == 0), stop=(f == KE - 1))
                    last.then_inc(op_done, 1)

            pe.wait_ge(w_loaded, 16 * 8)
            pe.wait_ge(setup_steps, 1)
            nc.tensor.matmul(ps[:, TR, 0:E], ones[0:1, 0:P], bv_row[:, :], start=True, stop=True)
            nc.tensor.matmul(ps[:, TR, E:2 * E], ones[0:1, 0:P], bo_row[:, :], start=True,
                             stop=True).then_inc(bias_rows_done, 1)
            pe.wait_ge(consts_ready, 3)
            pe.wait_ge(weights_ready, 1)
            transpose_xn(0, 1)
            pe.wait_ge(xt_copied, 1)
            transpose_xn(1, 2)
            with pe.Fori(0, B) as b:
                ln = b * N_LN
                pe.wait_ge(xt_copied, ln + 2)
                gate_up(b, 0, 0)
                gate_up(b, 0, 1)
                down(b, 0, 0)
                down(b, 0, 1)
                transpose_xn(0, ln + 3)
                pe.wait_ge(xt_copied, ln + 3)
                attention(b, 0)
                pe.wait_ge(res2_done, b * 4 + 2)
                transpose_xn(1, ln + 4)
                pe.wait_ge(xt_copied, ln + 4)
                attention(b, 1)
                pe.wait_ge(res2_done, b * 4 + 4)
                transpose_xn(0, ln + 5)
                pe.wait_ge(xt_copied, ln + 5)
                gate_up(b, 1, 0)
                transpose_xn(1, ln + 6)
                pe.wait_ge(xt_copied, ln + 6)
                gate_up(b, 1, 1)
                down(b, 1, 0)
                transpose_xn(0, ln + 7)
                down(b, 1, 1)
                pe.wait_ge(xt_copied, ln + 7)
                transpose_xn(1, ln + 8)


_OUT = ((B, L, E), "float32")


def kernel(**inputs):
    import numpy as np
    import concourse.bacc as bacc
    from concourse.bass_utils import run_bass_kernel_spmd

    a = {k: np.asarray(v) for k, v in inputs.items()}
    bias = a["L0_attn_qkv_b"]
    arrays = {
        "x": a["L0_attn_x"],
        "w_gate": a["L0_ffn_w_gate"].T,
        "w_up": a["L0_ffn_w_up"].T,
        "w_down": a["L0_ffn_w_down"].T,
        "w_qkv": a["L0_attn_qkv_w"],
        "b_cols": bias[:2 * E].reshape(4, P).T,
        "b_v": bias[2 * E:].reshape(1, E),
        "w_out": a["L0_attn_out_w"],
        "b_out": a["L0_attn_out_b"].reshape(1, E),
    }
    arrays = {k: np.ascontiguousarray(v) for k, v in arrays.items()}
    nc = bacc.Bacc("TRN2", target_bir_lowering=False, num_devices=1)
    args = [nc.dram_tensor(k, v.shape, mybir.dt.from_np(v.dtype), kind="ExternalInput").ap()
            for k, v in arrays.items()]
    args.append(nc.dram_tensor("out", _OUT[0], mybir.dt.from_np(np.dtype(_OUT[1])), kind="ExternalOutput").ap())
    build(nc, *args)
    r = run_bass_kernel_spmd(nc, [arrays], core_ids=[0])
    return r.results[0]["out"]
```

```python
from contextlib import ExitStack

import concourse.bass as bass
from concourse import mybir

FP32 = mybir.dt.float32
FP16 = mybir.dt.float16
I32 = mybir.dt.int32
ALU = mybir.AluOpType
ACT = mybir.ActivationFunctionType
AX = mybir.AxisListType

P = 128
B, L, E, H = 8, 1024, 256, 16
D = E // H
F = 768
HALF = L // 2
T = HALF // P
KE = E // P
KF = F // P
LN_EPS = 1e-5
DEN_EPS = 1e-6
W_SCALE = 1.0 / 127.0

XN_UP = 1024.0
H_UP = 0.5
W_UP = 1024.0
O_UP = 4.0
LIMITS = ((128.0, 0.0), (128.0, 0.0), (128.0, 0.0), (16.0, 2.0 ** -6), (16.0, 2.0 ** -6), (4096.0, 0.0))
NL = len(LIMITS)

BIG = 0
TR = 4
DOWN = 6
NUM = 6
STATE = 7

LAG = 2
NS = 2 * KF

N_LN = 6
N_GU = 4 * KF
N_DN = 8
N_CH = 2 * T
N_PROJ = 8
N_VP = 4


def build(nc, x, w_gate, w_up, w_down, w_qkv, b_cols, b_v, w_out, b_out, out):
    x_t = x.rearrange("b (h t p) e -> b h p t e", h=2, p=P)
    out_t = out.rearrange("b (h t p) e -> b h p t e", h=2, p=P)

    with ExitStack() as ctx:
        def sb(name, shape, dt=FP32):
            return ctx.enter_context(nc.sbuf_tensor(name, shape, dt))

        def sem(name):
            return ctx.enter_context(nc.semaphore(name))

        ps = ctx.enter_context(nc.psum_tensor("ps", [P, 8, 512], FP32))

        wg = sb("wg", [P, KE, F])
        wu = sb("wu", [P, KE, F])
        wd = sb("wd", [P, KF, E])
        wqkv = sb("wqkv", [P, KE, 3 * E])
        wo = sb("wo", [P, KE, E])
        bqk = sb("bqk", [P, 4])
        minus_bqk = sb("minus_bqk", [P, 4])
        bv_row = sb("bv_row", [1, E])
        bo_row = sb("bo_row", [1, E])
        bv = sb("bv", [P, E])
        bo = sb("bo", [P, E])
        ident = sb("ident", [P, P])
        causal = sb("causal", [P, P])
        same_head = sb("same_head", [P, P])
        parity = sb("parity", [P, 2])
        ones = sb("ones", [P, HALF])
        minus_half = sb("minus_half", [P, T])
        den_eps = sb("den_eps", [P, 1])
        wg16 = sb("wg16", [P, KE, F], FP16)
        wu16 = sb("wu16", [P, KE, F], FP16)
        wd16 = sb("wd16", [P, KF, E], FP16)
        wqkv16 = sb("wqkv16", [P, KE, 2, 3 * E], FP16)
        wo16 = sb("wo16", [P, KE, 2, E], FP16)
        largest = sb("largest", [P, NL])
        least = sb("least", [P, NL])
        absmax = sb("absmax", [P, NL])
        absmax_all = sb("absmax_all", [P, NL])
        upper = sb("upper", [1, NL])
        lower = sb("lower", [1, NL])
        below = sb("below", [1, NL])
        above = sb("above", [1, NL])
        within = sb("within", [1, NL])
        all_within = sb("all_within", [1, 1])
        use_split = sb("use_split", [1, 1], I32)
        xin = sb("xin", [P, 2, T, E])
        xr = sb("xr", [P, 2, T, E])
        xb = sb("xb", [P, 2, T, E])
        xn = sb("xn", [P, 2, T, E])
        xT = sb("xT", [P, 2, KE, HALF])
        stats = sb("stats", [P, T, 6])
        mean2 = sb("mean2", [P, T])
        gap = sb("gap", [P, T])
        gap2 = sb("gap2", [P, T])
        dev = sb("dev", [P, T])
        mean = sb("mean", [P, T])
        var_eps = sb("var_eps", [P, T])
        rstd = sb("rstd", [P, T])
        silu = sb("silu", [P, 2, HALF])
        hT = sb("hT", [P, 2, KF, HALF])
        h32 = sb("h32", [P, 2, HALF])
        elu_m = sb("elu_m", [P, 2, HALF])
        elu_e = sb("elu_e", [P, 2, HALF])
        elu_r = sb("elu_r", [P, 2, HALF])
        kT = sb("kT", [P, KE, HALF])
        qT = sb("qT", [P, KE, HALF])
        qz = sb("qz", [P, KE, 2, HALF])
        kcum = sb("kcum", [P, 2, KE, HALF])
        z = sb("z", [P, KE, HALF])
        k_tok = sb("k_tok", [P, T, E])
        v_tok = sb("v_tok", [P, T, H, 2 * D])
        scores = sb("scores", [P, 4, KE, 2, P])
        state = sb("state", [P, KE, P])
        den = sb("den", [P, KE, HALF])
        rden = sb("rden", [P, KE, HALF])
        oT = sb("oT", [P, KE, HALF])
        o32 = sb("o32", [P, KE, HALF])
        xT16 = xT[:, :, :, :].bitcast(FP16).rearrange("p h k (s n) -> p h k s n", s=2)
        hT16 = hT[:, :, :, :].bitcast(FP16).rearrange("p h k (s n) -> p h k s n", s=2)
        oT16 = oT[:, :, :].bitcast(FP16).rearrange("p k (s n) -> p k s n", s=2)

        w_loaded = sem("w_loaded")
        consts_ready = sem("consts_ready")
        setup_steps = sem("setup_steps")
        bias_rows_done = sem("bias_rows_done")
        weights_ready = sem("weights_ready")
        limits_ready = sem("limits_ready")
        absmax_ready = sem("absmax_ready")
        check_steps = sem("check_steps")
        branch_ready = sem("branch_ready")
        split_ready = sem("split_ready")
        x_loaded = [sem("x_loaded_a"), sem("x_loaded_b")]
        x_stored = [sem("x_stored_a"), sem("x_stored_b")]
        stats_done = sem("stats_done")
        sums_done = sem("sums_done")
        mean_done = sem("mean_done")
        var_ready = sem("var_ready")
        rstd_ready = sem("rstd_ready")
        xn_ready = sem("xn_ready")
        xt_done = sem("xt_done")
        xt_copied = sem("xt_copied")
        gu_done = sem("gu_done")
        silu_done = sem("silu_done")
        h_done = sem("h_done")
        h_hi_done = sem("h_hi_done")
        h_lo_done = sem("h_lo_done")
        xt_lo_done = sem("xt_lo_done")
        o_hi_done = sem("o_hi_done")
        o_lo_done = sem("o_lo_done")
        dn_done = sem("dn_done")
        res_done = sem("res_done")
        xb_done = sem("xb_done")
        vp_done = sem("vp_done")
        v_done = sem("v_done")
        proj_done = sem("proj_done")
        relu_done = sem("relu_done")
        elu_done = sem("elu_done")
        kq_done = sem("kq_done")
        kt_done = sem("kt_done")
        ktok_done = sem("ktok_done")
        qz_done = sem("qz_done")
        kcum_done = sem("kcum_done")
        z_done = sem("z_done")
        den_done = sem("den_done")
        den_copied = sem("den_copied")
        rden_done = sem("rden_done")
        s_done = sem("s_done")
        masked = sem("masked")
        ku_done = sem("ku_done")
        state_done = sem("state_done")
        pv_done = sem("pv_done")
        o_done = sem("o_done")
        op_done = sem("op_done")
        res2_done = sem("res2_done")

        block = ctx.enter_context(nc.Block())

        def either(eng, program):
            eng.wait_ge(branch_ready, 1)
            split = eng.value_load(use_split[0:1, 0:1], min_val=0, max_val=1)
            with eng.If(split == 0):
                program(False)
            with eng.Else():
                program(True)

        def v_heads(t, f):
            return v_tok[:, t, f * 8:f * 8 + 8, 0:D]

        def v_padded(t, h):
            flat = v_tok[:, t].rearrange("p h d -> p (h d)")
            at = 2 * D * h - D * (h % 2)
            return flat[:, at:at + 2 * D]

        @block.sync
        def _(sp):
            for dst, src in ((wg, w_gate), (wu, w_up), (wd, w_down)):
                sp.dma_start(dst[:, :, :].bitcast(I32), src.rearrange("(k p) n -> p k n", p=P)).then_inc(w_loaded, 16)
            for h in range(2):
                sp.dma_start(xin[:, h], x_t[0, h]).then_inc(x_loaded[h], 16)
            for dst, src in ((wqkv, w_qkv), (wo, w_out)):
                sp.dma_start(dst[:, :, :], src.rearrange("(k p) n -> p k n", p=P)).then_inc(w_loaded, 16)
            sp.dma_start(bqk[:, :], b_cols).then_inc(w_loaded, 16)
            sp.dma_start(bv_row[:, :], b_v).then_inc(w_loaded, 16)
            sp.dma_start(bo_row[:, :], b_out).then_inc(w_loaded, 16)
            with sp.Fori(1, B) as b:
                for h in range(2):
                    sp.wait_ge(res_done, b * N_DN + (2 * h + 2 + 2 - N_DN))
                    sp.dma_start(xin[:, h], x_t[b, h]).then_inc(x_loaded[h], 16)
                for h in range(2):
                    sp.wait_ge(res_done, b * N_DN + (4 + 2 * h + 2 + 2 - N_DN))
                    sp.dma_start(out_t[b - 1, h], xr[:, h]).then_inc(x_stored[h], 16)
            for h in range(2):
                sp.wait_ge(res_done, (B - 1) * N_DN + 2 * h + 2 + 2)
                sp.dma_start(xin[:, h], x_t[B - 1, h]).then_inc(x_loaded[h], 16)
            for h in range(2):
                sp.wait_ge(res_done, (B - 1) * N_DN + 4 + 2 * h + 2 + 2)
                sp.dma_start(out_t[B - 1, h], xr[:, h]).then_inc(x_stored[h], 16)
            for h in range(2):
                sp.wait_ge(x_stored[h], 16 * (B + 1))

        @block.gpsimd
        def _(pool):
            nc.gpsimd.memset(ident[:, :], 0.0)
            nc.gpsimd.memset(causal[:, :], 1.0)
            nc.gpsimd.memset(same_head[:, :], 1.0)
            nc.gpsimd.memset(minus_half[:, :], -0.5)
            nc.gpsimd.memset(den_eps[:, :], DEN_EPS).then_inc(consts_ready, 1)
            pool.wait_ge(consts_ready, 1)
            nc.gpsimd.affine_select(out=ident[:, :], in_=ident[:, :], compare_op=ALU.not_equal, fill=1.0,
                                    base=0, pattern=[[-1, P]], channel_multiplier=1)
            nc.gpsimd.affine_select(out=causal[:, :], in_=causal[:, :], compare_op=ALU.is_ge, fill=0.0,
                                    base=0, pattern=[[1, P]], channel_multiplier=-1)
            heads = same_head[:, :].rearrange("p (h d) -> p h d", d=D)
            nc.gpsimd.affine_select(out=heads, in_=heads, compare_op=ALU.is_ge, fill=0.0,
                                    base=0, pattern=[[-D, P // D], [0, D]], channel_multiplier=1).then_inc(consts_ready, 1)
            pool.wait_ge(consts_ready, 2)
            nc.gpsimd.affine_select(out=heads, in_=heads, compare_op=ALU.is_ge, fill=0.0,
                                    base=D - 1, pattern=[[D, P // D], [0, D]], channel_multiplier=-1).then_inc(consts_ready, 1)

            def pow_rstd(at):
                pool.wait_ge(var_ready, at)
                nc.gpsimd.tensor_tensor(rstd[:, :], var_eps[:, :], minus_half[:, :], ALU.pow).then_inc(rstd_ready, 1)

            def add_b_out(b, h):
                pool.wait_ge(res_done, b * N_DN + (2 * h + 2 + 2))
                nc.gpsimd.tensor_tensor(xb[:, h], xr[:, h], bo[:, :].unsqueeze(1).broadcast_to([P, T, E]),
                                        ALU.add).then_inc(xb_done, 1)

            def attention_in(b, h):
                for f in range(KE):
                    pool.wait_ge(kq_done, b * N_PROJ + (4 * h + f + 1 + 2))
                    for v in range(2):
                        last = nc.gpsimd.tensor_tensor(qz[:, f, v, :], qT[:, f, :],
                                                       parity[:, v:v + 1].broadcast_to([P, HALF]), ALU.mult)
                    last.then_inc(qz_done, 1)
                for f in range(KE):
                    pool.wait_ge(kcum_done, b * 4 + (2 * h + f + 1))
                    nc.gpsimd.tensor_tensor(z[:, f, :], qT[:, f, :], kcum[:, h, f, :], ALU.mult).then_inc(z_done, 1)

            def lo_of_h(split, b, ffn, tiles):
                if split:
                    for s in tiles:
                        pool.wait_ge(h_hi_done, b * N_GU + (NS * ffn + s + 1))
                        nc.gpsimd.tensor_tensor(hT16[:, s // KF, s % KF, 1, :], h32[:, s % 2, :],
                                                hT16[:, s // KF, s % KF, 0, :], ALU.subtract).then_inc(h_lo_done, 1)

            def lo_of_o(split, b, h, chunks):
                if split:
                    for c in chunks:
                        tok = slice(c * P, c * P + P)
                        pool.wait_ge(o_hi_done, b * N_CH + (T * h + c + 1))
                        nc.gpsimd.tensor_tensor(oT16[:, :, 1, tok], o32[:, :, tok], oT16[:, :, 0, tok],
                                                ALU.subtract).then_inc(o_lo_done, 1)

            def program(split):
                pow_rstd(1)
                pow_rstd(2)
                with pool.Fori(0, B) as b:
                    ln = b * N_LN
                    lo_of_h(split, b, 0, range(9))
                    pow_rstd(ln + 3)
                    lo_of_h(split, b, 0, range(9, NS))
                    attention_in(b, 0)
                    pow_rstd(ln + 4)
                    add_b_out(b, 0)
                    lo_of_o(split, b, 0, range(1))
                    add_b_out(b, 1)
                    lo_of_o(split, b, 0, range(1, T))
                    attention_in(b, 1)
                    pow_rstd(ln + 5)
                    lo_of_o(split, b, 1, range(T))
                    lo_of_h(split, b, 1, range(2))
                    pow_rstd(ln + 6)
                    lo_of_h(split, b, 1, range(2, 6))
                    pow_rstd(ln + 7)
                    lo_of_h(split, b, 1, range(6, 10))
                    pow_rstd(ln + 8)
                    lo_of_h(split, b, 1, range(10, NS))

            pool.wait_ge(limits_ready, 1)
            nc.gpsimd.partition_all_reduce(absmax_all[:, :], absmax[:, :], P,
                                           bass.bass_isa.ReduceOp.max).then_inc(absmax_ready, 1)
            pool.wait_ge(weights_ready, 1)
            either(pool, program)

        @block.scalar
        def _(act):
            def copy_xt(split, h, at):
                act.wait_ge(xt_done, at)
                dst = xT16[:, h, :, 0, :] if split else xT[:, h]
                nc.scalar.activation(dst, ps[:, TR:TR + KE, :], ACT.Copy).then_inc(xt_copied, 1)

            def hi_of_h(split, b, ffn, s):
                if split:
                    act.wait_ge(h_done, b * N_GU + (NS * ffn + s + 1 + 2))
                    nc.scalar.activation(hT16[:, s // KF, s % KF, 0, :], h32[:, s % 2, :],
                                         ACT.Copy).then_inc(h_hi_done, 1)

            def gate(split, b, ffn, tiles):
                c_gate = W_SCALE / (XN_UP if split else 1.0)
                for s in tiles:
                    n = NS * ffn + s
                    act.wait_ge(gu_done, b * N_GU + (n + 1))
                    act.wait_ge(h_done, b * N_GU + (n - 1 + 2))
                    nc.scalar.activation(silu[:, s % 2, :], ps[:, BIG + 2 * (s % 2), :], ACT.Silu,
                                         scale=c_gate).then_inc(silu_done, 1)
                    if s:
                        hi_of_h(split, b, ffn, s - 1)
                if s == NS - 1:
                    hi_of_h(split, b, ffn, s)

            def attention(split, b, h, next_h, next_ln):
                c_att = 1.0 / (XN_UP * W_UP) if split else 1.0
                for j in range(4):
                    bias = bqk[:, j:j + 1]
                    minus_bias = minus_bqk[:, j:j + 1]
                    act.wait_ge(proj_done, b * N_PROJ + (4 * h + j + 1))
                    act.wait_ge(kq_done, b * N_PROJ + (4 * h + j - 1 + 2))
                    nc.scalar.activation(elu_m[:, j % 2, :], ps[:, BIG + j, :], ACT.Relu, bias=minus_bias,
                                         scale=-c_att).then_inc(relu_done, 1)
                    nc.scalar.activation(elu_r[:, j % 2, :], ps[:, BIG + j, :], ACT.Relu, bias=bias, scale=c_att)
                    act.wait_ge(relu_done, b * N_PROJ + (4 * h + j + 1))
                    nc.scalar.activation(elu_e[:, j % 2, :], elu_m[:, j % 2, :], ACT.Exp,
                                         scale=-1.0).then_inc(elu_done, 1)
                for i in range(2):
                    act.wait_ge(kt_done, b * N_VP + (2 * h + i + 1))
                    nc.scalar.activation(k_tok[:, 2 * i:2 * i + 2, :],
                                         ps[:, TR + i, :].rearrange("p (t e) -> p t e", t=2),
                                         ACT.Copy).then_inc(ktok_done, 1)
                act.wait_ge(den_done, b * 2 + (h + 1))
                nc.scalar.activation(den[:, :, :], ps[:, TR:TR + KE, :], ACT.Identity,
                                     bias=den_eps[:, 0:1]).then_inc(den_copied, 1)
                for c in range(T):
                    if c == 2:
                        copy_xt(split, next_h, next_ln)
                    if split:
                        tok = slice(c * P, c * P + P)
                        act.wait_ge(o_done, b * N_CH + (T * h + c + 1))
                        nc.scalar.activation(oT16[:, :, 0, tok], o32[:, :, tok], ACT.Copy).then_inc(o_hi_done, 1)

            def program(split):
                copy_xt(split, 0, 1)
                copy_xt(split, 1, 2)
                with act.Fori(0, B) as b:
                    ln = b * N_LN
                    gate(split, b, 0, range(11))
                    copy_xt(split, 0, ln + 3)
                    gate(split, b, 0, range(11, NS))
                    attention(split, b, 0, 1, ln + 4)
                    attention(split, b, 1, 0, ln + 5)
                    gate(split, b, 1, range(5))
                    copy_xt(split, 1, ln + 6)
                    gate(split, b, 1, range(5, 9))
                    copy_xt(split, 0, ln + 7)
                    gate(split, b, 1, range(9, NS))
                    copy_xt(split, 1, ln + 8)

            act.wait_ge(consts_ready, 3)
            act.wait_ge(weights_ready, 1)
            either(act, program)

        @block.vector
        def _(dve):
            nc.vector.memset(ones[:, :], 1.0)
            nc.vector.memset(state[:, :, :], 0.0).then_inc(state_done, 1)
            nc.vector.memset(v_tok[:, :, :, :], 0.0).then_inc(setup_steps, 1)
            dve.wait_ge(w_loaded, 16 * 8)
            for w in (wg, wu):
                nc.vector.tensor_copy(w[:, :, :], w[:, :, :].bitcast(I32)).then_inc(h_done, 1)
            nc.vector.tensor_copy(wd[:, 0:3], wd[:, 0:3].bitcast(I32)).then_inc(res_done, 1)
            nc.vector.tensor_copy(wd[:, 3:6], wd[:, 3:6].bitcast(I32)).then_inc(res_done, 1)
            nc.vector.tensor_scalar(minus_bqk[:, :], bqk[:, :], -1.0, None, ALU.mult)
            dve.wait_ge(consts_ready, 3)
            for v in range(2):
                nc.vector.tensor_reduce(parity[:, v:v + 1], same_head[:, v * D:P:2 * D], AX.X, ALU.add).then_inc(kq_done, 1)
            dve.wait_ge(bias_rows_done, 1)
            nc.vector.tensor_copy(bv[:, :], ps[:, TR, 0:E])
            nc.vector.tensor_copy(bo[:, :], ps[:, TR, E:2 * E]).then_inc(weights_ready, 1)
            dve.wait_ge(weights_ready, 1)
            for i, w in enumerate((wg[:, :, :], wu[:, :, :], wd[:, :, :], wqkv[:, :, :], wo[:, :, :], bv[:, :])):
                axis = AX.XY if i < NL - 1 else AX.X
                nc.vector.tensor_reduce(largest[:, i:i + 1], w, axis, ALU.max)
                nc.vector.tensor_reduce(least[:, i:i + 1], w, axis, ALU.min)
            for i, (most, fewest) in enumerate(LIMITS):
                nc.vector.memset(upper[:, i:i + 1], most)
                last = nc.vector.memset(lower[:, i:i + 1], fewest)
            last.then_inc(check_steps, 1)
            dve.wait_ge(check_steps, 1)
            nc.vector.scalar_tensor_tensor(out=absmax[:, :], in0=least[:, :], scalar=-1.0, in1=largest[:, :],
                                           op0=ALU.mult, op1=ALU.max).then_inc(limits_ready, 1)
            dve.wait_ge(absmax_ready, 1)
            nc.vector.tensor_tensor(below[:, :], absmax_all[0:1, :], upper[:, :], ALU.is_le)
            nc.vector.tensor_tensor(above[:, :], absmax_all[0:1, :], lower[:, :], ALU.is_ge).then_inc(check_steps, 1)
            dve.wait_ge(check_steps, 2)
            nc.vector.tensor_tensor(within[:, :], below[:, :], above[:, :], ALU.mult).then_inc(check_steps, 1)
            dve.wait_ge(check_steps, 3)
            nc.vector.tensor_reduce(all_within[:, :], within[:, :], AX.X, ALU.min).then_inc(check_steps, 1)
            dve.wait_ge(check_steps, 4)
            nc.vector.tensor_copy(use_split[:, :], all_within[:, :]).then_inc(branch_ready, 1)

            def split_weights():
                for w, w16 in ((wg, wg16), (wu, wu16), (wd, wd16)):
                    nc.vector.tensor_copy(w16[:, :, :], w[:, :, :])
                for i, (w, w16) in enumerate(((wqkv, wqkv16), (wo, wo16))):
                    nc.vector.tensor_scalar(w16[:, :, 0, :], w[:, :, :], W_UP, None, ALU.mult).then_inc(check_steps, 1)
                    dve.wait_ge(check_steps, 5 + i)
                    last = nc.vector.scalar_tensor_tensor(out=w16[:, :, 1, :], in0=w[:, :, :], scalar=W_UP,
                                                          in1=w16[:, :, 0, :], op0=ALU.mult, op1=ALU.subtract)
                last.then_inc(split_ready, 1)

            def ln_stats(split, src, at, load=None):
                up = XN_UP if split else 1.0
                if load is not None:
                    dve.wait_ge(*load)
                for t in range(T):
                    last = nc.vector.bn_stats(stats[:, t, :], src[:, t, :])
                last.then_inc(stats_done, 1)
                dve.wait_ge(stats_done, at)
                mean_e, dev_e, mean_o, dev_o = (stats[:, :, i] for i in (1, 2, 4, 5))
                nc.vector.tensor_tensor(mean2[:, :], mean_e, mean_o, ALU.add)
                nc.vector.tensor_tensor(gap[:, :], mean_e, mean_o, ALU.subtract)
                nc.vector.scalar_tensor_tensor(out=dev[:, :], in0=dev_e, scalar=E * LN_EPS, in1=dev_o,
                                               op0=ALU.add, op1=ALU.add).then_inc(sums_done, 1)
                dve.wait_ge(sums_done, at)
                nc.vector.tensor_scalar(mean[:, :], mean2[:, :], 0.5, None, ALU.mult)
                nc.vector.scalar_tensor_tensor(out=gap2[:, :], in0=gap[:, :], scalar=0.25 / (up * up), in1=gap[:, :],
                                               op0=ALU.mult, op1=ALU.mult).then_inc(mean_done, 1)
                dve.wait_ge(mean_done, at)
                nc.vector.scalar_tensor_tensor(out=var_eps[:, :], in0=dev[:, :], scalar=1.0 / (E * up * up), in1=gap2[:, :],
                                               op0=ALU.mult, op1=ALU.add).then_inc(var_ready, 1)

            def ln_apply(src, h, at):
                dve.wait_ge(rstd_ready, at)
                dve.wait_ge(xt_done, at - 2)
                for t in range(T):
                    last = nc.vector.tensor_scalar(xn[:, h, t, :], src[:, t, :], mean[:, t:t + 1],
                                                   rstd[:, t:t + 1], ALU.subtract, ALU.mult)
                last.then_inc(xn_ready, 1)

            def lo_of_xt(split, h, at):
                if split:
                    dve.wait_ge(xt_copied, at)
                    nc.vector.tensor_tensor(xT16[:, h, :, 1, :], ps[:, TR:TR + KE, :], xT16[:, h, :, 0, :],
                                            ALU.subtract).then_inc(xt_lo_done, 1)

            def gate_times_up(split, b, ffn, tiles):
                c_up = W_SCALE * H_UP / XN_UP if split else W_SCALE
                for s in tiles:
                    n = NS * ffn + s
                    dve.wait_ge(silu_done, b * N_GU + (n + 1))
                    if split:
                        dve.wait_ge(h_lo_done, b * N_GU + (n - 1 + 2))
                    nc.vector.scalar_tensor_tensor(out=h32[:, s % 2, :] if split else hT[:, s // KF, s % KF, :],
                                                   in0=ps[:, BIG + 2 * (s % 2) + 1, :],
                                                   scalar=c_up, in1=silu[:, s % 2, :],
                                                   op0=ALU.mult, op1=ALU.mult).then_inc(h_done, 1)

            def residual(split, b, ffn, h):
                c_down = 0.5 * W_SCALE / (H_UP if split else 1.0)
                if ffn == 0:
                    dve.wait_ge(x_stored[h], b * 16 + 16)
                for i in range(2):
                    src = (xr if ffn else xin)[:, h, 2 * i:2 * i + 2, :]
                    dve.wait_ge(dn_done, b * N_DN + (4 * ffn + 2 * h + i + 1))
                    nc.vector.scalar_tensor_tensor(out=xr[:, h, 2 * i:2 * i + 2, :],
                                                   in0=ps[:, DOWN + i, :].rearrange("p (t e) -> p t e", t=2),
                                                   scalar=c_down, in1=src,
                                                   op0=ALU.mult, op1=ALU.add).then_inc(res_done, 1)

            def q_or_k(b, h, tiles):
                for j in tiles:
                    dst = (qT, kT)[j // 2][:, j % 2, :]
                    dve.wait_ge(elu_done, b * N_PROJ + (4 * h + j + 1))
                    nc.vector.tensor_tensor(dst, elu_e[:, j % 2, :], elu_r[:, j % 2, :], ALU.add).then_inc(kq_done, 1)

            def v_and_scan(split, b, h):
                c_att = 1.0 / (XN_UP * W_UP) if split else 1.0
                for i in range(2):
                    dve.wait_ge(vp_done, b * N_VP + (2 * h + i + 1))
                    for t in (2 * i, 2 * i + 1):
                        last = nc.vector.scalar_tensor_tensor(
                            out=v_tok[:, t, :, 0:D],
                            in0=ps[:, TR + i, (t % 2) * E:(t % 2) * E + E].rearrange("p (h d) -> p h d", d=D),
                            scalar=c_att, in1=bv[:, :].rearrange("p (h d) -> p h d", d=D),
                            op0=ALU.mult, op1=ALU.add)
                    last.then_inc(v_done, 1)
                for f in range(KE):
                    dve.wait_ge(kq_done, b * N_PROJ + (4 * h + 2 + f + 1 + 2))
                    if h:
                        dve.wait_ge(kcum_done, b * 4 + (f + 1))
                    nc.vector.tensor_tensor_scan(kcum[:, h, f, :], ones[:, :], kT[:, f, :],
                                                 kcum[:, 0, f, HALF - 1:HALF] if h else 0.0,
                                                 ALU.mult, ALU.add).then_inc(kcum_done, 1)

            def attention_chunks(split, b, h, ln, next_h):
                o = o32 if split else oT
                for c in range(T):
                    n = T * h + c
                    for i in range(2):
                        dve.wait_ge(s_done, b * 2 * N_CH + (2 * n + i + 1))
                        nc.vector.tensor_tensor(
                            scores[:, 2 * i:2 * i + 2].rearrange("p g f v q -> p (g f v) q"),
                            ps[:, BIG + 2 * i:BIG + 2 * i + 2, :].rearrange("p g (x q) -> p (g x) q", q=P),
                            causal[:, :].unsqueeze(1).broadcast_to([P, 8, P]), ALU.mult).then_inc(masked, 1)
                    if n < N_CH - 1:
                        dve.wait_ge(ku_done, b * (N_CH - 1) + (n + 1))
                        nc.vector.tensor_tensor(state[:, :, :],
                                                ps[:, STATE, 0:KE * P].rearrange("p (f e) -> p f e", f=KE),
                                                same_head[:, :].unsqueeze(1).broadcast_to([P, KE, P]),
                                                ALU.mult).then_inc(state_done, 1)
                    tok = slice(c * P, c * P + P)
                    if c == 0:
                        ln_apply(xr[:, next_h], next_h, ln)
                        dve.wait_ge(den_copied, b * 2 + (h + 1))
                    if c == 2:
                        lo_of_xt(split, next_h, ln)
                    nc.vector.reciprocal(rden[:, :, tok], den[:, :, tok]).then_inc(rden_done, 1)
                    dve.wait_ge(rden_done, b * N_CH + (n + 1))
                    dve.wait_ge(pv_done, b * N_CH + (n + 1))
                    nc.vector.scalar_tensor_tensor(out=o[:, :, tok],
                                                   in0=ps[:, NUM, 0:KE * P].rearrange("p (f q) -> p f q", f=KE),
                                                   scalar=O_UP if split else 1.0, in1=rden[:, :, tok],
                                                   op0=ALU.mult, op1=ALU.mult).then_inc(o_done, 1)
                if h:
                    nc.vector.memset(state[:, :, :], 0.0).then_inc(state_done, 1)

            def attention_residual(split, b, h):
                c_op = 1.0 / (O_UP * W_UP) if split else 1.0
                dve.wait_ge(xb_done, b * 2 + (h + 1))
                for i in range(2):
                    dve.wait_ge(op_done, b * N_VP + (2 * h + i + 1))
                    nc.vector.scalar_tensor_tensor(out=xr[:, h, 2 * i:2 * i + 2, :],
                                                   in0=ps[:, TR + i, :].rearrange("p (t e) -> p t e", t=2),
                                                   scalar=c_op, in1=xb[:, h, 2 * i:2 * i + 2, :],
                                                   op0=ALU.mult, op1=ALU.add).then_inc(res2_done, 1)

            def own_residual(b, ffn, h):
                dve.wait_ge(res_done, b * N_DN + (4 * ffn + 2 * h + 2 + 2))

            nc.vector.memset(xb[:, 0, 0, 0:1], 0.0).then_inc(x_stored[0], 16)
            nc.vector.memset(xb[:, 1, 0, 0:1], 0.0).then_inc(x_stored[1], 16)

            def program(split):
                if split:
                    nc.vector.memset(h32[:, 0, 0:1], 0.0).then_inc(h_lo_done, 1)
                    nc.vector.memset(h32[:, 1, 0:1], 0.0).then_inc(h_lo_done, 1)
                    split_weights()
                for h in range(2):
                    ln_stats(split, xin[:, h], h + 1, (x_loaded[h], 16))
                    dve.wait_ge(rstd_ready, h + 1)
                    for t in range(T):
                        last = nc.vector.tensor_scalar(xn[:, h, t, :], xin[:, h, t, :], mean[:, t:t + 1],
                                                       rstd[:, t:t + 1], ALU.subtract, ALU.mult)
                    last.then_inc(xn_ready, 1)
                    lo_of_xt(split, h, h + 1)
                with dve.Fori(0, B) as b:
                    ln = b * N_LN
                    gate_times_up(split, b, 0, range(8))
                    residual(split, b, 0, 0)
                    gate_times_up(split, b, 0, range(8, 9))
                    own_residual(b, 0, 0)
                    ln_stats(split, xr[:, 0], ln + 3)
                    gate_times_up(split, b, 0, range(9, 10))
                    ln_apply(xr[:, 0], 0, ln + 3)
                    gate_times_up(split, b, 0, range(10, 11))
                    lo_of_xt(split, 0, ln + 3)
                    gate_times_up(split, b, 0, range(11, NS))
                    q_or_k(b, 0, range(2))
                    residual(split, b, 0, 1)
                    q_or_k(b, 0, range(2, 4))
                    v_and_scan(split, b, 0)
                    own_residual(b, 0, 1)
                    ln_stats(split, xr[:, 1], ln + 4)
                    attention_chunks(split, b, 0, ln + 4, 1)
                    q_or_k(b, 1, range(2))
                    attention_residual(split, b, 0)
                    q_or_k(b, 1, range(2, 4))
                    v_and_scan(split, b, 1)
                    dve.wait_ge(res2_done, b * 4 + 2)
                    ln_stats(split, xr[:, 0], ln + 5)
                    attention_chunks(split, b, 1, ln + 5, 0)
                    gate_times_up(split, b, 1, range(2))
                    attention_residual(split, b, 1)
                    dve.wait_ge(res2_done, b * 4 + 4)
                    ln_stats(split, xr[:, 1], ln + 6)
                    gate_times_up(split, b, 1, range(2, 3))
                    ln_apply(xr[:, 1], 1, ln + 6)
                    gate_times_up(split, b, 1, range(3, 5))
                    lo_of_xt(split, 1, ln + 6)
                    gate_times_up(split, b, 1, range(5, 6))
                    ln_stats(split, xin[:, 0], ln + 7, (x_loaded[0], b * 16 + 32))
                    gate_times_up(split, b, 1, range(6, 7))
                    ln_apply(xin[:, 0], 0, ln + 7)
                    gate_times_up(split, b, 1, range(7, 8))
                    residual(split, b, 1, 0)
                    gate_times_up(split, b, 1, range(8, 9))
                    lo_of_xt(split, 0, ln + 7)
                    gate_times_up(split, b, 1, range(9, 10))
                    ln_stats(split, xin[:, 1], ln + 8, (x_loaded[1], b * 16 + 32))
                    gate_times_up(split, b, 1, range(10, 11))
                    ln_apply(xin[:, 1], 1, ln + 8)
                    gate_times_up(split, b, 1, range(11, NS))
                    lo_of_xt(split, 1, ln + 8)
                    residual(split, b, 1, 1)

            either(dve, program)

        @block.tensor
        def _(pe):
            HI, LO = 0, 1

            def product(dst, terms):
                for i, (stationary, moving) in enumerate(terms):
                    last = nc.tensor.matmul(dst, stationary, moving, start=(i == 0), stop=(i == len(terms) - 1))
                return last

            def transpose_xn(h, at):
                pe.wait_ge(xn_ready, at)
                for f in range(KE):
                    for t in range(T):
                        last = nc.tensor.transpose(ps[:, TR + f, t * P:t * P + P],
                                                   xn[:, h, t, f * P:f * P + P], ident[:, :])
                last.then_inc(xt_done, 1)

            def gate_up(split, b, ffn, s):
                h, m = divmod(s, KF)
                pe.wait_ge(h_done, b * N_GU + (NS * ffn + s - 1 + 2))
                cols = slice(m * P, m * P + P)
                for j in range(2):
                    if split:
                        w = (wg16, wu16)[j]
                        terms = [(w[:, k, cols], xT16[:, h, k, r, :]) for k in range(KE) for r in (HI, LO)]
                    else:
                        w = (wg, wu)[j]
                        terms = [(w[:, k, cols], xT[:, h, k, :]) for k in range(KE)]
                    last = product(ps[:, BIG + 2 * (s % 2) + j, :], terms)
                last.then_inc(gu_done, 1)

            def down(split, b, ffn, s):
                h, k = divmod(s, KF)
                pe.wait_ge(h_lo_done if split else h_done, b * N_GU + (NS * ffn + s + 1 + 2))
                for i in range(2):
                    if k == 0:
                        pe.wait_ge(res_done, b * N_DN + (4 * ffn + 2 * h + i - 1 + 2))
                    for t in (2 * i, 2 * i + 1):
                        tok = slice(t * P, t * P + P)
                        dst = ps[:, DOWN + i, (t % 2) * E:(t % 2) * E + E]
                        parts = [hT16[:, h, k, r, tok] for r in (HI, LO)] if split else [hT[:, h, k, tok]]
                        for r, part in enumerate(parts):
                            last = nc.tensor.matmul(dst, part, (wd16 if split else wd)[:, k, :],
                                                    start=(k == 0 and r == 0 and t % 2 == 0), stop=(k == KF - 1),
                                                    skip_group_check=True)
                    if k == KF - 1:
                        last.then_inc(dn_done, 1)

            pairs = ((HI, HI), (HI, LO), (LO, HI))

            def q_or_k(split, h, j):
                col = j * P
                if split:
                    terms = [(wqkv16[:, k, s, col:col + P], xT16[:, h, k, r, :])
                             for k in range(KE) for s, r in pairs]
                else:
                    terms = [(wqkv[:, k, col:col + P], xT[:, h, k, :]) for k in range(KE)]
                product(ps[:, BIG + j, :], terms).then_inc(proj_done, 1)

            def q_or_k_after_ffn(split, b):
                for j in range(4):
                    if j % 2 == 0:
                        pe.wait_ge(h_done, b * N_GU + (NS - LAG + j // 2 + 1 + 2))
                    q_or_k(split, 0, j)
                    if j < LAG:
                        down(split, b, 0, NS - LAG + j)

            def v_and_k(split, b, h):
                for i in range(2):
                    for t in (2 * i, 2 * i + 1):
                        tok = slice(t * P, t * P + P)
                        if split:
                            terms = [(xT16[:, h, k, s, tok], wqkv16[:, k, r, 2 * E:3 * E])
                                     for k in range(KE) for s, r in pairs]
                        else:
                            terms = [(xT[:, h, k, tok], wqkv[:, k, 2 * E:3 * E]) for k in range(KE)]
                        last = product(ps[:, TR + i, (t % 2) * E:(t % 2) * E + E], terms)
                    last.then_inc(vp_done, 1)
                pe.wait_ge(kq_done, b * N_PROJ + (4 * h + 4 + 2))
                for i in range(2):
                    pe.wait_ge(v_done, b * N_VP + (2 * h + i + 1))
                    for t in (2 * i, 2 * i + 1):
                        for f in range(KE):
                            last = nc.tensor.transpose(ps[:, TR + i, (t % 2) * E + f * P:(t % 2) * E + f * P + P],
                                                       kT[:, f, t * P:t * P + P], ident[:, :])
                    last.then_inc(kt_done, 1)

            def chunks(b, h, next_h, next_ln):
                pe.wait_ge(qz_done, b * 4 + (2 * h + 2))
                for c in range(T):
                    n = T * h + c
                    tok = slice(c * P, c * P + P)
                    for i in range(2):
                        for g in (2 * i, 2 * i + 1):
                            rows = slice(32 * g, 32 * g + 32)
                            for f in range(KE):
                                last = nc.tensor.matmul(ps[:, BIG + g, f * 2 * P:(f + 1) * 2 * P],
                                                        kT[rows, f, tok], qz[rows, f, :, tok],
                                                        start=True, stop=True)
                        last.then_inc(s_done, 1)
                    pe.wait_ge(state_done, b * N_CH + (n + 1))
                    if n == 0:
                        pe.wait_ge(res_done, b * N_DN + (4 + 2))
                    else:
                        pe.wait_ge(o_done, b * N_CH + n)
                    for f in range(KE):
                        nc.tensor.matmul(ps[:, NUM, f * P:f * P + P], state[:, f, :], qT[:, f, tok],
                                         start=(f == 0), stop=False, skip_group_check=True)
                    if c == 0:
                        pe.wait_ge(ktok_done, b * N_VP + (2 * h + 2))
                    if n < N_CH - 1:
                        for f in range(KE):
                            last = nc.tensor.matmul(ps[:, STATE, f * P:f * P + P], k_tok[:, c, f * P:f * P + P],
                                                    v_heads(c, f), start=(n == 0 and f == 0), stop=True,
                                                    skip_group_check=True)
                        last.then_inc(ku_done, 1)
                    if c == 0:
                        pe.wait_ge(z_done, b * 4 + (2 * h + 2))
                        for f in range(KE):
                            last = nc.tensor.matmul(ps[:, TR + f, :], same_head[:, :], z[:, f, :],
                                                    start=True, stop=True)
                        last.then_inc(den_done, 1)
                    if c == 2:
                        pe.wait_ge(den_copied, b * 2 + (h + 1))
                        transpose_xn(next_h, next_ln)
                    for i in range(2):
                        pe.wait_ge(masked, b * 2 * N_CH + (2 * n + i + 1))
                        for g in (2 * i, 2 * i + 1):
                            for f in range(KE):
                                for v in range(2):
                                    last = nc.tensor.matmul(ps[32 * g:32 * g + 32, NUM, f * P:f * P + P],
                                                            v_padded(c, 8 * f + 2 * g + v),
                                                            scores[:, g, f, v, :], start=False, stop=True,
                                                            skip_group_check=True)
                    last.then_inc(pv_done, 1)

            def output(split, b, h):
                for i in range(2):
                    for t in (2 * i, 2 * i + 1):
                        tok = slice(t * P, t * P + P)
                        pe.wait_ge(o_lo_done if split else o_done, b * N_CH + (T * h + t + 1))
                        if split:
                            terms = [(oT16[:, f, s, tok], wo16[:, f, r, :]) for f in range(KE) for s, r in pairs]
                        else:
                            terms = [(oT[:, f, tok], wo[:, f, :]) for f in range(KE)]
                        last = product(ps[:, TR + i, (t % 2) * E:(t % 2) * E + E], terms)
                    last.then_inc(op_done, 1)

            pe.wait_ge(w_loaded, 16 * 8)
            pe.wait_ge(setup_steps, 1)
            nc.tensor.matmul(ps[:, TR, 0:E], ones[0:1, 0:P], bv_row[:, :], start=True, stop=True)
            nc.tensor.matmul(ps[:, TR, E:2 * E], ones[0:1, 0:P], bo_row[:, :], start=True,
                             stop=True).then_inc(bias_rows_done, 1)
            pe.wait_ge(consts_ready, 3)
            pe.wait_ge(weights_ready, 1)

            def program(split):
                xt_ready = xt_lo_done if split else xt_copied
                if split:
                    pe.wait_ge(split_ready, 1)
                transpose_xn(0, 1)
                pe.wait_ge(xt_ready, 1)
                transpose_xn(1, 2)
                with pe.Fori(0, B) as b:
                    ln = b * N_LN
                    pe.wait_ge(xt_ready, ln + 2)
                    for s in range(NS):
                        gate_up(split, b, 0, s)
                        if s >= LAG:
                            down(split, b, 0, s - LAG)
                        if s == 10:
                            transpose_xn(0, ln + 3)
                    pe.wait_ge(xt_ready, ln + 3)
                    q_or_k_after_ffn(split, b)
                    v_and_k(split, b, 0)
                    chunks(b, 0, 1, ln + 4)
                    pe.wait_ge(xt_ready, ln + 4)
                    q_or_k(split, 1, 0)
                    q_or_k(split, 1, 1)
                    output(split, b, 0)
                    q_or_k(split, 1, 2)
                    q_or_k(split, 1, 3)
                    pe.wait_ge(res2_done, b * 4 + 2)
                    v_and_k(split, b, 1)
                    chunks(b, 1, 0, ln + 5)
                    pe.wait_ge(xt_ready, ln + 5)
                    for s in range(NS):
                        if s == KF:
                            pe.wait_ge(xt_ready, ln + 6)
                        gate_up(split, b, 1, s)
                        if s == 1:
                            output(split, b, 1)
                        if s >= LAG:
                            down(split, b, 1, s - LAG)
                        if s == 4:
                            transpose_xn(1, ln + 6)
                        if s == 8:
                            transpose_xn(0, ln + 7)
                    pe.wait_ge(xt_ready, ln + 7)
                    transpose_xn(1, ln + 8)
                    for s in range(NS - LAG, NS):
                        down(split, b, 1, s)

            either(pe, program)


_OUT = ((B, L, E), "float32")


def kernel(**inputs):
    import numpy as np
    import concourse.bacc as bacc
    from concourse.bass_utils import run_bass_kernel_spmd

    a = {k: np.asarray(v) for k, v in inputs.items()}
    bias = a["L0_attn_qkv_b"]
    arrays = {
        "x": a["L0_attn_x"],
        "w_gate": a["L0_ffn_w_gate"].T,
        "w_up": a["L0_ffn_w_up"].T,
        "w_down": a["L0_ffn_w_down"].T,
        "w_qkv": a["L0_attn_qkv_w"],
        "b_cols": bias[:2 * E].reshape(4, P).T,
        "b_v": bias[2 * E:].reshape(1, E),
        "w_out": a["L0_attn_out_w"],
        "b_out": a["L0_attn_out_b"].reshape(1, E),
    }
    arrays = {k: np.ascontiguousarray(v) for k, v in arrays.items()}
    nc = bacc.Bacc("TRN2", target_bir_lowering=False, num_devices=1)
    args = [nc.dram_tensor(k, v.shape, mybir.dt.from_np(v.dtype), kind="ExternalInput").ap()
            for k, v in arrays.items()]
    args.append(nc.dram_tensor("out", _OUT[0], mybir.dt.from_np(np.dtype(_OUT[1])), kind="ExternalOutput").ap())
    build(nc, *args)
    r = run_bass_kernel_spmd(nc, [arrays], core_ids=[0])
    return r.results[0]["out"]
```

```python
from contextlib import ExitStack

import concourse.bass as bass
from concourse import mybir

FP32 = mybir.dt.float32
FP16 = mybir.dt.float16
I32 = mybir.dt.int32
ALU = mybir.AluOpType
ACT = mybir.ActivationFunctionType
AX = mybir.AxisListType

P = 128
B, L, E, H = 8, 1024, 256, 16
D = E // H
F = 768
HALF = L // 2
T = HALF // P
KE = E // P
KF = F // P
LN_EPS = 1e-5
DEN_EPS = 1e-6
W_SCALE = 1.0 / 127.0

XN_UP = 1024.0
H_UP = 0.5
W_UP = 1024.0
O_UP = 4.0
LIMITS = ((128.0, 0.0), (128.0, 0.0), (128.0, 0.0), (16.0, 2.0 ** -6), (16.0, 2.0 ** -6), (4096.0, 0.0))
NL = len(LIMITS)

BIG = 0
TR = 4
DOWN = 6
NUM = 6
STATE = 7

LAG = 2
NS = 2 * KF

N_LN = 6
N_GU = 4 * KF
N_DN = 8
N_CH = 2 * T
N_PROJ = 8
N_VP = 4


def build(nc, x, w_gate, w_up, w_down, w_qkv, b_cols, b_v, w_out, b_out, out):
    x_t = x.rearrange("b (h t p) e -> b h p t e", h=2, p=P)
    out_t = out.rearrange("b (h t p) e -> b h p t e", h=2, p=P)

    with ExitStack() as ctx:
        def sb(name, shape, dt=FP32):
            return ctx.enter_context(nc.sbuf_tensor(name, shape, dt))

        def sem(name):
            return ctx.enter_context(nc.semaphore(name))

        ps = ctx.enter_context(nc.psum_tensor("ps", [P, 8, 512], FP32))

        wg = sb("wg", [P, KE, F])
        wu = sb("wu", [P, KE, F])
        wd = sb("wd", [P, KF, E])
        wqkv = sb("wqkv", [P, KE, 3 * E])
        wo = sb("wo", [P, KE, E])
        bqk = sb("bqk", [P, 4])
        minus_bqk = sb("minus_bqk", [P, 4])
        bqk_up = sb("bqk_up", [P, 4])
        bv_row = sb("bv_row", [1, E])
        bo_row = sb("bo_row", [1, E])
        bv = sb("bv", [P, E])
        bo = sb("bo", [P, E])
        ident = sb("ident", [P, P])
        ident16 = sb("ident16", [P, P], FP16)
        causal = sb("causal", [P, P])
        same_head = sb("same_head", [P, P])
        parity = sb("parity", [P, 2])
        ones = sb("ones", [P, HALF])
        minus_half = sb("minus_half", [P, T])
        den_eps = sb("den_eps", [P, 1])
        wg16 = sb("wg16", [P, KE, F], FP16)
        wu16 = sb("wu16", [P, KE, F], FP16)
        wd16 = sb("wd16", [P, KF, E], FP16)
        wqkv16 = sb("wqkv16", [P, KE, 2, 3 * E], FP16)
        wo16 = sb("wo16", [P, KE, 2, E], FP16)
        absmax = sb("absmax", [P, NL])
        absmax_all = sb("absmax_all", [P, NL])
        upper = sb("upper", [1, NL])
        lower = sb("lower", [1, NL])
        below = sb("below", [1, NL])
        above = sb("above", [1, NL])
        within = sb("within", [1, NL])
        spare_exp = sb("spare_exp", [P, 1])
        spare = sb("spare", [P, 10])
        all_within = sb("all_within", [1, 1])
        use_split = sb("use_split", [1, 1], I32)
        xin = sb("xin", [P, 2, T, E])
        xr = sb("xr", [P, 2, T, E])
        xb = sb("xb", [P, 2, T, E])
        xn = sb("xn", [P, T, E])
        xn16 = sb("xn16", [P, T, 2, E], FP16)
        xT = sb("xT", [P, 2, KE, HALF])
        stats = sb("stats", [P, T, 6])
        mean2 = sb("mean2", [P, T])
        gap = sb("gap", [P, T])
        gap2 = sb("gap2", [P, T])
        dev = sb("dev", [P, T])
        mean = sb("mean", [P, T])
        var_eps = sb("var_eps", [P, T])
        rstd = sb("rstd", [P, T])
        silu = sb("silu", [P, 2, HALF])
        hT = sb("hT", [P, 2, KF, HALF])
        h32 = sb("h32", [P, 2, HALF])
        elu_m = sb("elu_m", [P, 2, HALF])
        elu_e = sb("elu_e", [P, 2, HALF])
        elu_r = sb("elu_r", [P, 2, HALF])
        kT = sb("kT", [P, KE, HALF])
        qT = sb("qT", [P, KE, HALF])
        qz = sb("qz", [P, KE, 2, HALF])
        kcum = sb("kcum", [P, 2, KE, HALF])
        z = sb("z", [P, KE, HALF])
        k_tok = sb("k_tok", [P, T, E])
        v_tok = sb("v_tok", [P, T, H, 2 * D])
        scores = sb("scores", [P, 4, KE, 2, P])
        state = sb("state", [P, KE, P])
        den = sb("den", [P, KE, HALF])
        rden = sb("rden", [P, KE, HALF])
        oT = sb("oT", [P, KE, HALF])
        o32 = sb("o32", [P, KE, HALF])
        xT16 = xT[:, :, :, :].bitcast(FP16).rearrange("p h k (s n) -> p h k s n", s=2)
        hT16 = hT[:, :, :, :].bitcast(FP16).rearrange("p h k (s n) -> p h k s n", s=2)
        oT16 = oT[:, :, :].bitcast(FP16).rearrange("p k (s n) -> p k s n", s=2)
        tr16 = ps[:, TR:TR + 2, :].bitcast(FP16).rearrange("p s (f n) -> p s f n", f=KE)

        ffn_w_loaded = [sem("w_gate_loaded"), sem("w_up_loaded"), sem("w_down_loaded")]
        att_w_loaded = [sem("w_qkv_loaded"), sem("w_out_loaded")]
        biases_loaded = sem("biases_loaded")
        ffn_w_ready = sem("ffn_w_ready")
        consts_ready = sem("consts_ready")
        setup_steps = sem("setup_steps")
        bias_rows_done = sem("bias_rows_done")
        bias_ready = sem("bias_ready")
        limits_ready = sem("limits_ready")
        absmax_ready = sem("absmax_ready")
        check_steps = sem("check_steps")
        branch_ready = sem("branch_ready")
        bqk_up_ready = sem("bqk_up_ready")
        att_hi_done = sem("att_hi_done")
        wg16_ready = sem("wg16_ready")
        wd16_ready = sem("wd16_ready")
        split_ready = sem("split_ready")
        x_loaded = [sem("x_loaded_a"), sem("x_loaded_b")]
        x_stored = [sem("x_stored_a"), sem("x_stored_b")]
        stats_done = sem("stats_done")
        sums_done = sem("sums_done")
        mean_done = sem("mean_done")
        var_ready = sem("var_ready")
        rstd_ready = sem("rstd_ready")
        xn_ready = sem("xn_ready")
        xn_hi_done = sem("xn_hi_done")
        xn_lo_done = sem("xn_lo_done")
        xt_done = sem("xt_done")
        xt_copied = sem("xt_copied")
        gu_done = sem("gu_done")
        silu_done = sem("silu_done")
        h_done = sem("h_done")
        h_hi_done = sem("h_hi_done")
        h_lo_done = sem("h_lo_done")
        xt_lo_done = sem("xt_lo_done")
        o_hi_done = sem("o_hi_done")
        o_lo_done = sem("o_lo_done")
        dn_done = sem("dn_done")
        res_done = sem("res_done")
        xb_done = sem("xb_done")
        vp_done = sem("vp_done")
        v_done = sem("v_done")
        proj_done = sem("proj_done")
        relu_done = sem("relu_done")
        min_done = sem("min_done")
        elu_done = sem("elu_done")
        kq_done = sem("kq_done")
        kt_done = sem("kt_done")
        ktok_done = sem("ktok_done")
        qz_done = sem("qz_done")
        kcum_done = sem("kcum_done")
        z_done = sem("z_done")
        den_done = sem("den_done")
        den_copied = sem("den_copied")
        rden_done = sem("rden_done")
        s_done = sem("s_done")
        masked = sem("masked")
        ku_done = sem("ku_done")
        state_done = sem("state_done")
        pv_done = sem("pv_done")
        o_done = sem("o_done")
        op_done = sem("op_done")
        res2_done = sem("res2_done")

        block = ctx.enter_context(nc.Block())

        def either(eng, program):
            eng.wait_ge(branch_ready, 1)
            split = eng.value_load(use_split[0:1, 0:1], min_val=0, max_val=1)
            with eng.If(split == 0):
                program(False)
            with eng.Else():
                program(True)

        def v_heads(t, f):
            return v_tok[:, t, f * 8:f * 8 + 8, 0:D]

        def v_padded(t, h):
            flat = v_tok[:, t].rearrange("p h d -> p (h d)")
            at = 2 * D * h - D * (h % 2)
            return flat[:, at:at + 2 * D]

        @block.sync
        def _(sp):
            def load_ffn(i, dst, src):
                sp.dma_start(dst[:, :, :].bitcast(I32),
                             src.rearrange("(k p) n -> p k n", p=P)).then_inc(ffn_w_loaded[i], 16)

            sp.dma_start(xin[:, 0], x_t[0, 0]).then_inc(x_loaded[0], 16)
            load_ffn(0, wg, w_gate)
            sp.dma_start(bqk[:, :], b_cols).then_inc(biases_loaded, 16)
            sp.dma_start(bv_row[:, :], b_v).then_inc(biases_loaded, 16)
            sp.dma_start(bo_row[:, :], b_out).then_inc(biases_loaded, 16)
            load_ffn(1, wu, w_up)
            load_ffn(2, wd, w_down)
            for i, (dst, src) in enumerate(((wqkv, w_qkv), (wo, w_out))):
                sp.dma_start(dst[:, :, :], src.rearrange("(k p) n -> p k n", p=P)).then_inc(att_w_loaded[i], 16)
            sp.dma_start(xin[:, 1], x_t[0, 1]).then_inc(x_loaded[1], 16)
            with sp.Fori(1, B) as b:
                for h in range(2):
                    sp.wait_ge(res_done, b * N_DN + (2 * h + 2 + 2 - N_DN))
                    sp.dma_start(xin[:, h], x_t[b, h]).then_inc(x_loaded[h], 16)
                for h in range(2):
                    sp.wait_ge(res_done, b * N_DN + (4 + 2 * h + 2 + 2 - N_DN))
                    sp.dma_start(out_t[b - 1, h], xr[:, h]).then_inc(x_stored[h], 16)
            sp.wait_ge(res_done, (B - 1) * N_DN + 2 + 2)
            sp.dma_start(xin[:, 0], x_t[B - 1, 0]).then_inc(x_loaded[0], 16)
            for h in range(2):
                sp.wait_ge(res_done, (B - 1) * N_DN + 4 + 2 * h + 2 + 2)
                sp.dma_start(out_t[B - 1, h], xr[:, h]).then_inc(x_stored[h], 16)
            for h in range(2):
                sp.wait_ge(x_stored[h], 16 * (B + 1))

        @block.gpsimd
        def _(pool):
            nc.gpsimd.memset(ident[:, :], 0.0)
            nc.gpsimd.memset(causal[:, :], 1.0)
            nc.gpsimd.memset(same_head[:, :], 1.0)
            nc.gpsimd.memset(minus_half[:, :], -0.5)
            nc.gpsimd.memset(den_eps[:, :], DEN_EPS).then_inc(consts_ready, 1)
            pool.wait_ge(consts_ready, 1)
            nc.gpsimd.affine_select(out=ident[:, :], in_=ident[:, :], compare_op=ALU.not_equal, fill=1.0,
                                    base=0, pattern=[[-1, P]], channel_multiplier=1)
            nc.gpsimd.affine_select(out=causal[:, :], in_=causal[:, :], compare_op=ALU.is_ge, fill=0.0,
                                    base=0, pattern=[[1, P]], channel_multiplier=-1)
            heads = same_head[:, :].rearrange("p (h d) -> p h d", d=D)
            nc.gpsimd.affine_select(out=heads, in_=heads, compare_op=ALU.is_ge, fill=0.0,
                                    base=0, pattern=[[-D, P // D], [0, D]], channel_multiplier=1).then_inc(consts_ready, 1)
            pool.wait_ge(consts_ready, 2)
            nc.gpsimd.affine_select(out=heads, in_=heads, compare_op=ALU.is_ge, fill=0.0,
                                    base=D - 1, pattern=[[D, P // D], [0, D]], channel_multiplier=-1).then_inc(consts_ready, 1)

            def pow_rstd(at):
                pool.wait_ge(var_ready, at)
                nc.gpsimd.tensor_tensor(rstd[:, :], var_eps[:, :], minus_half[:, :], ALU.pow).then_inc(rstd_ready, 1)

            def add_b_out(b, h):
                pool.wait_ge(res_done, b * N_DN + (2 * h + 2 + 2))
                nc.gpsimd.tensor_tensor(xb[:, h], xr[:, h], bo[:, :].unsqueeze(1).broadcast_to([P, T, E]),
                                        ALU.add).then_inc(xb_done, 1)

            def attention_in(b, h):
                for f in range(KE):
                    pool.wait_ge(kq_done, b * N_PROJ + (4 * h + f + 1 + 2))
                    for v in range(2):
                        last = nc.gpsimd.tensor_tensor(qz[:, f, v, :], qT[:, f, :],
                                                       parity[:, v:v + 1].broadcast_to([P, HALF]), ALU.mult)
                    last.then_inc(qz_done, 1)
                for f in range(KE):
                    pool.wait_ge(kcum_done, b * 4 + (2 * h + f + 1))
                    nc.gpsimd.tensor_tensor(z[:, f, :], qT[:, f, :], kcum[:, h, f, :], ALU.mult).then_inc(z_done, 1)

            def lo_of_h(split, b, ffn, tiles):
                if split:
                    for s in tiles:
                        pool.wait_ge(h_hi_done, b * N_GU + (NS * ffn + s + 1))
                        nc.gpsimd.tensor_tensor(hT16[:, s // KF, s % KF, 1, :], h32[:, s % 2, :],
                                                hT16[:, s // KF, s % KF, 0, :], ALU.subtract).then_inc(h_lo_done, 1)

            def lo_of_o(split, b, h, chunks):
                if split:
                    for c in chunks:
                        tok = slice(c * P, c * P + P)
                        pool.wait_ge(o_hi_done, b * N_CH + (T * h + c + 1))
                        nc.gpsimd.tensor_tensor(oT16[:, :, 1, tok], o32[:, :, tok], oT16[:, :, 0, tok],
                                                ALU.subtract).then_inc(o_lo_done, 1)

            def program(split):
                with pool.Fori(0, B) as b:
                    ln = b * N_LN
                    lo_of_h(split, b, 0, range(1))
                    pow_rstd(ln + 2)
                    lo_of_h(split, b, 0, range(1, 8))
                    pow_rstd(ln + 3)
                    lo_of_h(split, b, 0, range(8, NS))
                    attention_in(b, 0)
                    pow_rstd(ln + 4)
                    add_b_out(b, 0)
                    lo_of_o(split, b, 0, range(1))
                    add_b_out(b, 1)
                    lo_of_o(split, b, 0, range(1, T))
                    attention_in(b, 1)
                    pow_rstd(ln + 5)
                    lo_of_o(split, b, 1, range(T))
                    lo_of_h(split, b, 1, range(2))
                    pow_rstd(ln + 6)
                    lo_of_h(split, b, 1, range(2, 7))
                    pow_rstd(ln + 7)
                    lo_of_h(split, b, 1, range(7, NS))

            pow_rstd(1)
            pool.wait_ge(ffn_w_ready, 1)
            nc.gpsimd.tensor_scalar(wg16[:, :, :], wg[:, :, :], LIMITS[0][0], -LIMITS[0][0], ALU.min,
                                    ALU.max).then_inc(wg16_ready, 1)
            pool.wait_ge(limits_ready, 1)
            nc.gpsimd.partition_all_reduce(absmax_all[:, :], absmax[:, :], P,
                                           bass.bass_isa.ReduceOp.max).then_inc(absmax_ready, 1)
            either(pool, program)

        @block.scalar
        def _(act):
            def copy_xt(split, h, at):
                act.wait_ge(xt_done, at)
                if split:
                    nc.scalar.activation(xT16[:, h, :, 0, :], tr16[:, 0], ACT.Copy).then_inc(xt_copied, 1)
                else:
                    nc.scalar.activation(xT[:, h], ps[:, TR:TR + KE, :], ACT.Copy).then_inc(xt_copied, 1)

            def hi_of_xn(split, at):
                if split:
                    act.wait_ge(xn_ready, at)
                    nc.scalar.activation(xn16[:, :, 0, :], xn[:, :, :], ACT.Copy).then_inc(xn_hi_done, 1)

            def hi_of_h(split, b, ffn, s):
                if split:
                    act.wait_ge(h_done, b * N_GU + (NS * ffn + s + 1 + 2))
                    nc.scalar.activation(hT16[:, s // KF, s % KF, 0, :], h32[:, s % 2, :],
                                         ACT.Copy).then_inc(h_hi_done, 1)

            def gate(split, b, ffn, tiles, xn_at=None, copy=None):
                c_gate = W_SCALE / XN_UP
                for s in tiles:
                    n = NS * ffn + s
                    act.wait_ge(gu_done, b * N_GU + (n + 1))
                    act.wait_ge(h_done, b * N_GU + (n - 1 + 2))
                    nc.scalar.activation(silu[:, s % 2, :], ps[:, BIG + 2 * (s % 2), :], ACT.Silu,
                                         scale=c_gate).then_inc(silu_done, 1)
                    if s == tiles[-1] and xn_at is not None:
                        hi_of_xn(split, xn_at)
                    if s == tiles[-1] and copy is not None:
                        copy_xt(split, *copy)
                    hi_of_h(split, b, ffn, s)

            def attention(split, b, h, next_h, next_ln):
                c_att = 1.0 / (XN_UP * (W_UP if split else 1.0))
                for j in range(4):
                    bias = bqk[:, j:j + 1]
                    minus_bias = minus_bqk[:, j:j + 1]
                    act.wait_ge(proj_done, b * N_PROJ + (4 * h + j + 1))
                    act.wait_ge(kq_done, b * N_PROJ + (4 * h + j - 1 + 2))
                    if j % 2 == 0:
                        nc.scalar.activation(elu_m[:, 0, :], ps[:, BIG + j, :], ACT.Relu, bias=minus_bias,
                                             scale=-c_att).then_inc(relu_done, 1)
                    else:
                        act.wait_ge(min_done, b * 4 + (2 * h + j // 2 + 1))
                    nc.scalar.activation(elu_r[:, j % 2, :], ps[:, BIG + j, :], ACT.Relu, bias=bias, scale=c_att)
                    if j % 2 == 0:
                        act.wait_ge(relu_done, b * 4 + (2 * h + j // 2 + 1))
                    nc.scalar.activation(elu_e[:, j % 2, :], elu_m[:, j % 2, :], ACT.Exp,
                                         scale=c_att if j % 2 else -1.0).then_inc(elu_done, 1)
                for i in range(2):
                    act.wait_ge(kt_done, b * N_VP + (2 * h + i + 1))
                    nc.scalar.activation(k_tok[:, 2 * i:2 * i + 2, :],
                                         ps[:, TR + i, :].rearrange("p (t e) -> p t e", t=2),
                                         ACT.Copy).then_inc(ktok_done, 1)
                act.wait_ge(den_done, b * 2 + (h + 1))
                nc.scalar.activation(den[:, :, :], ps[:, TR:TR + KE, :], ACT.Identity,
                                     bias=den_eps[:, 0:1]).then_inc(den_copied, 1)
                hi_of_xn(split, next_ln)
                for c in range(T):
                    if c == 2:
                        copy_xt(split, next_h, next_ln)
                    if split:
                        tok = slice(c * P, c * P + P)
                        act.wait_ge(o_done, b * N_CH + (T * h + c + 1))
                        nc.scalar.activation(oT16[:, :, 0, tok], o32[:, :, tok], ACT.Copy).then_inc(o_hi_done, 1)

            def program(split):
                copy_xt(split, 0, 1)
                if split:
                    for w, w16 in ((wqkv, wqkv16), (wo, wo16)):
                        nc.scalar.activation(w16[:, :, 0, :], w[:, :, :], ACT.Copy, scale=W_UP).then_inc(att_hi_done, 1)
                with act.Fori(0, B) as b:
                    ln = b * N_LN
                    gate(split, b, 0, range(3), xn_at=ln + 2)
                    gate(split, b, 0, range(3, 5))
                    copy_xt(split, 1, ln + 2)
                    gate(split, b, 0, range(5, 10), xn_at=ln + 3)
                    gate(split, b, 0, range(10, NS), copy=(0, ln + 3))
                    nc.scalar.activation(spare_exp[:, 0:1], den_eps[:, 0:1], ACT.Exp)
                    attention(split, b, 0, 1, ln + 4)
                    attention(split, b, 1, 0, ln + 5)
                    gate(split, b, 1, range(4), xn_at=ln + 6)
                    gate(split, b, 1, range(4, 6), copy=(1, ln + 6))
                    gate(split, b, 1, range(6, 9), xn_at=ln + 7)
                    gate(split, b, 1, range(9, NS))
                    copy_xt(split, 0, ln + 7)

            def float32_of(i, w):
                act.wait_ge(ffn_w_loaded[i], 16)
                nc.scalar.activation(w[:, :, :], w[:, :, :].bitcast(I32), ACT.Copy).then_inc(ffn_w_ready, 1)

            float32_of(0, wg)
            float32_of(1, wu)
            hi_of_xn(True, 1)
            float32_of(2, wd)
            either(act, program)

        @block.vector
        def _(dve):
            def lo_of_attention_weights():
                for i, (w, w16) in enumerate(((wqkv, wqkv16), (wo, wo16))):
                    dve.wait_ge(att_hi_done, i + 1)
                    last = nc.vector.scalar_tensor_tensor(out=w16[:, :, 1, :], in0=w[:, :, :], scalar=W_UP,
                                                          in1=w16[:, :, 0, :], op0=ALU.mult, op1=ALU.subtract)
                last.then_inc(split_ready, 1)

            def ln_moments(src, load=None):
                if load is not None:
                    dve.wait_ge(*load)
                for t in range(T):
                    last = nc.vector.bn_stats(stats[:, t, :], src[:, t, :])
                last.then_inc(stats_done, 1)

            def ln_variance(at):
                up = XN_UP
                dve.wait_ge(stats_done, at)
                mean_e, dev_e, mean_o, dev_o = (stats[:, :, i] for i in (1, 2, 4, 5))
                nc.vector.tensor_tensor(mean2[:, :], mean_e, mean_o, ALU.add)
                nc.vector.tensor_tensor(gap[:, :], mean_e, mean_o, ALU.subtract)
                nc.vector.scalar_tensor_tensor(out=dev[:, :], in0=dev_e, scalar=E * LN_EPS, in1=dev_o,
                                               op0=ALU.add, op1=ALU.add).then_inc(sums_done, 1)
                dve.wait_ge(sums_done, at)
                nc.vector.tensor_scalar(mean[:, :], mean2[:, :], 0.5, None, ALU.mult)
                nc.vector.scalar_tensor_tensor(out=gap2[:, :], in0=gap[:, :], scalar=0.25 / (up * up), in1=gap[:, :],
                                               op0=ALU.mult, op1=ALU.mult).then_inc(mean_done, 1)
                dve.wait_ge(mean_done, at)
                nc.vector.scalar_tensor_tensor(out=var_eps[:, :], in0=dev[:, :], scalar=1.0 / (E * up * up), in1=gap2[:, :],
                                               op0=ALU.mult, op1=ALU.add).then_inc(var_ready, 1)

            def ln_stats(src, at, load=None):
                ln_moments(src, load)
                ln_variance(at)

            def ln_apply(src, at, before=None):
                dve.wait_ge(rstd_ready, at)
                if before is not None:
                    dve.wait_ge(xt_done, before)
                for t in range(T):
                    last = nc.vector.tensor_scalar(xn[:, t, :], src[:, t, :], mean[:, t:t + 1],
                                                   rstd[:, t:t + 1], ALU.subtract, ALU.mult)
                last.then_inc(xn_ready, 1)

            def lo_of_xn(split, at):
                if split:
                    dve.wait_ge(xn_hi_done, at)
                    nc.vector.tensor_tensor(xn16[:, :, 1, :], xn[:, :, :], xn16[:, :, 0, :],
                                            ALU.subtract).then_inc(xn_lo_done, 1)

            def lo_of_xt(split, h, at):
                if split:
                    dve.wait_ge(xt_done, at)
                    nc.vector.tensor_copy(xT16[:, h, :, 1, :], tr16[:, 1]).then_inc(xt_lo_done, 1)

            def gate_times_up(split, b, ffn, tiles):
                c_up = W_SCALE * (H_UP if split else 1.0) / XN_UP
                for s in tiles:
                    n = NS * ffn + s
                    dve.wait_ge(silu_done, b * N_GU + (n + 1))
                    if split:
                        dve.wait_ge(h_lo_done, b * N_GU + (n - 1 + 2))
                    nc.vector.scalar_tensor_tensor(out=h32[:, s % 2, :] if split else hT[:, s // KF, s % KF, :],
                                                   in0=ps[:, BIG + 2 * (s % 2) + 1, :],
                                                   scalar=c_up, in1=silu[:, s % 2, :],
                                                   op0=ALU.mult, op1=ALU.mult).then_inc(h_done, 1)

            def residual(split, b, ffn, h):
                c_down = 0.5 * W_SCALE / (H_UP if split else 1.0)
                if ffn == 0:
                    dve.wait_ge(x_stored[h], b * 16 + 16)
                for i in range(2):
                    src = (xr if ffn else xin)[:, h, 2 * i:2 * i + 2, :]
                    dve.wait_ge(dn_done, b * N_DN + (4 * ffn + 2 * h + i + 1))
                    nc.vector.scalar_tensor_tensor(out=xr[:, h, 2 * i:2 * i + 2, :],
                                                   in0=ps[:, DOWN + i, :].rearrange("p (t e) -> p t e", t=2),
                                                   scalar=c_down, in1=src,
                                                   op0=ALU.mult, op1=ALU.add).then_inc(res_done, 1)

            def min_of(b, h, j):
                dve.wait_ge(proj_done, b * N_PROJ + (4 * h + j + 1))
                nc.vector.tensor_scalar(elu_m[:, 1, :], ps[:, BIG + j, :], bqk_up[:, j:j + 1], 0.0,
                                        ALU.add, ALU.min).then_inc(min_done, 1)

            def q_or_k(b, h, tiles):
                for j in tiles:
                    dst = (qT, kT)[j // 2][:, j % 2, :]
                    dve.wait_ge(elu_done, b * N_PROJ + (4 * h + j + 1))
                    nc.vector.tensor_tensor(dst, elu_e[:, j % 2, :], elu_r[:, j % 2, :], ALU.add).then_inc(kq_done, 1)

            def v_bank(split, b, h, i):
                c_att = 1.0 / (XN_UP * (W_UP if split else 1.0))
                dve.wait_ge(vp_done, b * N_VP + (2 * h + i + 1))
                for t in (2 * i, 2 * i + 1):
                    last = nc.vector.scalar_tensor_tensor(
                        out=v_tok[:, t, :, 0:D],
                        in0=ps[:, TR + i, (t % 2) * E:(t % 2) * E + E].rearrange("p (h d) -> p h d", d=D),
                        scalar=c_att, in1=bv[:, :].rearrange("p (h d) -> p h d", d=D),
                        op0=ALU.mult, op1=ALU.add)
                last.then_inc(v_done, 1)

            def k_and_v(split, b, h):
                min_of(b, h, 3)
                q_or_k(b, h, range(2, 3))
                v_bank(split, b, h, 0)
                q_or_k(b, h, range(3, 4))
                v_bank(split, b, h, 1)

            def scan(b, h):
                for f in range(KE):
                    dve.wait_ge(kq_done, b * N_PROJ + (4 * h + 2 + f + 1 + 2))
                    if h:
                        dve.wait_ge(kcum_done, b * 4 + (f + 1))
                    nc.vector.tensor_tensor_scan(kcum[:, h, f, :], ones[:, :], kT[:, f, :],
                                                 kcum[:, 0, f, HALF - 1:HALF] if h else 0.0,
                                                 ALU.mult, ALU.add).then_inc(kcum_done, 1)

            def attention_chunks(split, b, h, ln, next_h):
                o = o32 if split else oT
                for c in range(T):
                    n = T * h + c
                    for i in range(2):
                        dve.wait_ge(s_done, b * 2 * N_CH + (2 * n + i + 1))
                        nc.vector.tensor_tensor(
                            scores[:, 2 * i:2 * i + 2].rearrange("p g f v q -> p (g f v) q"),
                            ps[:, BIG + 2 * i:BIG + 2 * i + 2, :].rearrange("p g (x q) -> p (g x) q", q=P),
                            causal[:, :].unsqueeze(1).broadcast_to([P, 8, P]), ALU.mult).then_inc(masked, 1)
                    if n < N_CH - 1:
                        dve.wait_ge(ku_done, b * (N_CH - 1) + (n + 1))
                        nc.vector.tensor_tensor(state[:, :, :],
                                                ps[:, STATE, 0:KE * P].rearrange("p (f e) -> p f e", f=KE),
                                                same_head[:, :].unsqueeze(1).broadcast_to([P, KE, P]),
                                                ALU.mult).then_inc(state_done, 1)
                    tok = slice(c * P, c * P + P)
                    if c == 0:
                        ln_apply(xr[:, next_h], ln, ln - 1)
                        dve.wait_ge(den_copied, b * 2 + (h + 1))
                    if c == 1:
                        lo_of_xn(split, ln)
                    if c == 2:
                        lo_of_xt(split, next_h, ln)
                    nc.vector.reciprocal(rden[:, :, tok], den[:, :, tok]).then_inc(rden_done, 1)
                    dve.wait_ge(rden_done, b * N_CH + (n + 1))
                    dve.wait_ge(pv_done, b * N_CH + (n + 1))
                    nc.vector.scalar_tensor_tensor(out=o[:, :, tok],
                                                   in0=ps[:, NUM, 0:KE * P].rearrange("p (f q) -> p f q", f=KE),
                                                   scalar=O_UP if split else 1.0, in1=rden[:, :, tok],
                                                   op0=ALU.mult, op1=ALU.mult).then_inc(o_done, 1)
                if h:
                    nc.vector.memset(state[:, :, :], 0.0).then_inc(state_done, 1)

            def attention_residual(split, b, h):
                c_op = 1.0 / (O_UP * W_UP) if split else 1.0
                dve.wait_ge(xb_done, b * 2 + (h + 1))
                for i in range(2):
                    dve.wait_ge(op_done, b * N_VP + (2 * h + i + 1))
                    nc.vector.scalar_tensor_tensor(out=xr[:, h, 2 * i:2 * i + 2, :],
                                                   in0=ps[:, TR + i, :].rearrange("p (t e) -> p t e", t=2),
                                                   scalar=c_op, in1=xb[:, h, 2 * i:2 * i + 2, :],
                                                   op0=ALU.mult, op1=ALU.add).then_inc(res2_done, 1)

            def own_residual(b, ffn, h):
                dve.wait_ge(res_done, b * N_DN + (4 * ffn + 2 * h + 2 + 2))

            nc.vector.memset(ones[:, :], 1.0).then_inc(setup_steps, 1)
            nc.vector.memset(state[:, :, :], 0.0).then_inc(state_done, 1)
            nc.vector.memset(v_tok[:, :, :, :], 0.0)
            for i, (most, fewest) in enumerate(LIMITS):
                nc.vector.memset(upper[:, i:i + 1], most)
                nc.vector.memset(lower[:, i:i + 1], fewest)
            for i, free in enumerate((h_done, h_lo_done, res_done, kq_done)):
                for j in range(2):
                    nc.vector.memset(spare[:, 2 * i + j:2 * i + j + 1], 0.0).then_inc(free, 1)
            for h in range(2):
                nc.vector.memset(spare[:, 8 + h:9 + h], 0.0).then_inc(x_stored[h], 16)
            dve.wait_ge(consts_ready, 3)
            nc.vector.tensor_copy(ident16[:, :], ident[:, :])
            for v in range(2):
                nc.vector.tensor_reduce(parity[:, v:v + 1], same_head[:, v * D:P:2 * D], AX.X, ALU.add)
            ln_stats(xin[:, 0], 1, (x_loaded[0], 16))
            def largest(i, w):
                return nc.vector.tensor_reduce(absmax[:, i:i + 1], w, AX.XY if i < NL - 1 else AX.X, ALU.max,
                                               apply_absolute_value=True)

            dve.wait_ge(ffn_w_ready, 1)
            largest(0, wg[:, :, :])
            dve.wait_ge(biases_loaded, 16 * 3)
            nc.vector.tensor_scalar(minus_bqk[:, :], bqk[:, :], -1.0, None, ALU.mult)
            dve.wait_ge(bias_rows_done, 1)
            nc.vector.tensor_copy(bv[:, :], ps[:, TR, 0:E])
            nc.vector.tensor_copy(bo[:, :], ps[:, TR, E:2 * E]).then_inc(bias_ready, 1)
            ln_apply(xin[:, 0], 1)
            dve.wait_ge(ffn_w_ready, 2)
            largest(1, wu[:, :, :])
            nc.vector.tensor_scalar(wu16[:, :, :], wu[:, :, :], LIMITS[1][0], -LIMITS[1][0], ALU.min, ALU.max)
            lo_of_xn(True, 1)
            dve.wait_ge(bias_ready, 1)
            largest(NL - 1, bv[:, :])
            dve.wait_ge(ffn_w_ready, 3)
            largest(2, wd[:, :, :])
            dve.wait_ge(att_w_loaded[0], 16)
            largest(3, wqkv[:, :, :])
            dve.wait_ge(att_w_loaded[1], 16)
            last = largest(4, wo[:, :, :])
            last.then_inc(limits_ready, 1)
            dve.wait_ge(absmax_ready, 1)
            nc.vector.tensor_tensor(below[:, :], absmax_all[0:1, :], upper[:, :], ALU.is_le)
            nc.vector.tensor_tensor(above[:, :], absmax_all[0:1, :], lower[:, :], ALU.is_ge).then_inc(check_steps, 1)
            dve.wait_ge(check_steps, 1)
            nc.vector.tensor_tensor(within[:, :], below[:, :], above[:, :], ALU.mult).then_inc(check_steps, 1)
            dve.wait_ge(check_steps, 2)
            nc.vector.tensor_reduce(all_within[:, :], within[:, :], AX.X, ALU.min).then_inc(check_steps, 1)
            dve.wait_ge(check_steps, 3)
            nc.vector.tensor_copy(use_split[:, :], all_within[:, :]).then_inc(branch_ready, 1)

            def program(split):
                nc.vector.tensor_scalar(bqk_up[:, :], bqk[:, :], XN_UP * (W_UP if split else 1.0), None,
                                        ALU.mult).then_inc(bqk_up_ready, 1)
                dve.wait_ge(bqk_up_ready, 1)
                lo_of_xt(split, 0, 1)
                if split:
                    nc.vector.tensor_copy(wd16[:, :, :], wd[:, :, :]).then_inc(wd16_ready, 1)
                    lo_of_attention_weights()
                with dve.Fori(0, B) as b:
                    ln = b * N_LN
                    gate_times_up(split, b, 0, range(1))
                    ln_stats(xin[:, 1], ln + 2, (x_loaded[1], b * 16 + 16))
                    gate_times_up(split, b, 0, range(1, 2))
                    ln_apply(xin[:, 1], ln + 2, ln + 1)
                    gate_times_up(split, b, 0, range(2, 3))
                    lo_of_xn(split, ln + 2)
                    gate_times_up(split, b, 0, range(3, 5))
                    lo_of_xt(split, 1, ln + 2)
                    gate_times_up(split, b, 0, range(5, 8))
                    residual(split, b, 0, 0)
                    own_residual(b, 0, 0)
                    ln_stats(xr[:, 0], ln + 3)
                    gate_times_up(split, b, 0, range(8, 9))
                    ln_apply(xr[:, 0], ln + 3, ln + 2)
                    gate_times_up(split, b, 0, range(9, 10))
                    lo_of_xn(split, ln + 3)
                    gate_times_up(split, b, 0, range(10, NS))
                    lo_of_xt(split, 0, ln + 3)
                    q_or_k(b, 0, range(1))
                    min_of(b, 0, 1)
                    residual(split, b, 0, 1)
                    q_or_k(b, 0, range(1, 2))
                    k_and_v(split, b, 0)
                    scan(b, 0)
                    own_residual(b, 0, 1)
                    ln_stats(xr[:, 1], ln + 4)
                    attention_chunks(split, b, 0, ln + 4, 1)
                    q_or_k(b, 1, range(1))
                    min_of(b, 1, 1)
                    q_or_k(b, 1, range(1, 2))
                    attention_residual(split, b, 0)
                    k_and_v(split, b, 1)
                    scan(b, 1)
                    dve.wait_ge(res2_done, b * 4 + 2)
                    ln_stats(xr[:, 0], ln + 5)
                    attention_chunks(split, b, 1, ln + 5, 0)
                    gate_times_up(split, b, 1, range(2))
                    attention_residual(split, b, 1)
                    dve.wait_ge(res2_done, b * 4 + 4)
                    ln_stats(xr[:, 1], ln + 6)
                    gate_times_up(split, b, 1, range(2, 3))
                    ln_apply(xr[:, 1], ln + 6, ln + 5)
                    gate_times_up(split, b, 1, range(3, 4))
                    lo_of_xn(split, ln + 6)
                    gate_times_up(split, b, 1, range(4, 6))
                    lo_of_xt(split, 1, ln + 6)
                    ln_moments(xin[:, 0], (x_loaded[0], b * 16 + 32))
                    gate_times_up(split, b, 1, range(6, 7))
                    ln_variance(ln + 7)
                    gate_times_up(split, b, 1, range(7, 8))
                    residual(split, b, 1, 0)
                    ln_apply(xin[:, 0], ln + 7, ln + 6)
                    gate_times_up(split, b, 1, range(8, 9))
                    lo_of_xn(split, ln + 7)
                    gate_times_up(split, b, 1, range(9, NS))
                    lo_of_xt(split, 0, ln + 7)
                    residual(split, b, 1, 1)

            either(dve, program)

        @block.tensor
        def _(pe):
            HI, LO = 0, 1

            def product(dst, terms):
                for i, (stationary, moving) in enumerate(terms):
                    last = nc.tensor.matmul(dst, stationary, moving, start=(i == 0), stop=(i == len(terms) - 1))
                return last

            def transpose_xn(split, at):
                if split:
                    pe.wait_ge(xn_lo_done, at)
                    for r in (HI, LO):
                        for f in range(KE):
                            for t in range(T):
                                last = nc.tensor.transpose(tr16[:, r, f, t * P:t * P + P],
                                                           xn16[:, t, r, f * P:f * P + P], ident16[:, :])
                else:
                    pe.wait_ge(xn_ready, at)
                    for f in range(KE):
                        for t in range(T):
                            last = nc.tensor.transpose(ps[:, TR + f, t * P:t * P + P],
                                                       xn[:, t, f * P:f * P + P], ident[:, :])
                last.then_inc(xt_done, 1)

            def wait_xt(split, at):
                pe.wait_ge(xt_copied, at)
                if split:
                    pe.wait_ge(xt_lo_done, at)

            def gate_up(split, b, ffn, s):
                h, m = divmod(s, KF)
                pe.wait_ge(h_done, b * N_GU + (NS * ffn + s - 1 + 2))
                cols = slice(m * P, m * P + P)
                for j in range(2):
                    if split:
                        w = (wg16, wu16)[j]
                        terms = [(w[:, k, cols], xT16[:, h, k, r, :]) for k in range(KE) for r in (HI, LO)]
                    else:
                        w = (wg, wu)[j]
                        terms = [(w[:, k, cols], xT[:, h, k, :]) for k in range(KE)]
                    last = product(ps[:, BIG + 2 * (s % 2) + j, :], terms)
                last.then_inc(gu_done, 1)

            def down(split, b, ffn, s):
                h, k = divmod(s, KF)
                if split and ffn == 0 and s == 0:
                    pe.wait_ge(wd16_ready, 1)
                pe.wait_ge(h_lo_done if split else h_done, b * N_GU + (NS * ffn + s + 1 + 2))
                for i in range(2):
                    if k == 0:
                        pe.wait_ge(res_done, b * N_DN + (4 * ffn + 2 * h + i - 1 + 2))
                    for t in (2 * i, 2 * i + 1):
                        tok = slice(t * P, t * P + P)
                        dst = ps[:, DOWN + i, (t % 2) * E:(t % 2) * E + E]
                        parts = [hT16[:, h, k, r, tok] for r in (HI, LO)] if split else [hT[:, h, k, tok]]
                        for r, part in enumerate(parts):
                            last = nc.tensor.matmul(dst, part, (wd16 if split else wd)[:, k, :],
                                                    start=(k == 0 and r == 0 and t % 2 == 0), stop=(k == KF - 1),
                                                    skip_group_check=True)
                    if k == KF - 1:
                        last.then_inc(dn_done, 1)

            pairs = ((HI, HI), (HI, LO), (LO, HI))

            def q_or_k(split, h, j):
                col = j * P
                if split:
                    terms = [(wqkv16[:, k, s, col:col + P], xT16[:, h, k, r, :])
                             for k in range(KE) for s, r in pairs]
                else:
                    terms = [(wqkv[:, k, col:col + P], xT[:, h, k, :]) for k in range(KE)]
                product(ps[:, BIG + j, :], terms).then_inc(proj_done, 1)

            def q_or_k_after_ffn(split, b):
                for j in range(4):
                    if j % 2 == 0:
                        pe.wait_ge(h_done, b * N_GU + (NS - LAG + j // 2 + 1 + 2))
                    q_or_k(split, 0, j)
                    if j == 0:
                        down(split, b, 0, NS - 1)

            def v_and_k(split, b, h):
                for i in range(2):
                    for t in (2 * i, 2 * i + 1):
                        tok = slice(t * P, t * P + P)
                        if split:
                            terms = [(xT16[:, h, k, s, tok], wqkv16[:, k, r, 2 * E:3 * E])
                                     for k in range(KE) for s, r in pairs]
                        else:
                            terms = [(xT[:, h, k, tok], wqkv[:, k, 2 * E:3 * E]) for k in range(KE)]
                        last = product(ps[:, TR + i, (t % 2) * E:(t % 2) * E + E], terms)
                    last.then_inc(vp_done, 1)
                pe.wait_ge(kq_done, b * N_PROJ + (4 * h + 4 + 2))
                for i in range(2):
                    pe.wait_ge(v_done, b * N_VP + (2 * h + i + 1))
                    for t in (2 * i, 2 * i + 1):
                        for f in range(KE):
                            last = nc.tensor.transpose(ps[:, TR + i, (t % 2) * E + f * P:(t % 2) * E + f * P + P],
                                                       kT[:, f, t * P:t * P + P], ident[:, :])
                    last.then_inc(kt_done, 1)

            def chunks(split, b, h, next_ln):
                pe.wait_ge(qz_done, b * 4 + (2 * h + 2))
                for c in range(T):
                    n = T * h + c
                    tok = slice(c * P, c * P + P)
                    for i in range(2):
                        for f in range(KE):
                            for g in (2 * i, 2 * i + 1):
                                rows = slice(32 * g, 32 * g + 32)
                                last = nc.tensor.matmul(ps[:, BIG + g, f * 2 * P:(f + 1) * 2 * P],
                                                        kT[rows, f, tok], qz[rows, f, :, tok],
                                                        start=True, stop=True)
                        last.then_inc(s_done, 1)
                    pe.wait_ge(state_done, b * N_CH + (n + 1))
                    if n == 0:
                        pe.wait_ge(res_done, b * N_DN + (4 + 2))
                    else:
                        pe.wait_ge(o_done, b * N_CH + n)
                    for f in range(KE):
                        nc.tensor.matmul(ps[:, NUM, f * P:f * P + P], state[:, f, :], qT[:, f, tok],
                                         start=(f == 0), stop=False, skip_group_check=True)
                    if c == 0:
                        pe.wait_ge(ktok_done, b * N_VP + (2 * h + 2))
                    if n < N_CH - 1:
                        for f in range(KE):
                            last = nc.tensor.matmul(ps[:, STATE, f * P:f * P + P], k_tok[:, c, f * P:f * P + P],
                                                    v_heads(c, f), start=(n == 0 and f == 0), stop=True,
                                                    skip_group_check=True)
                        last.then_inc(ku_done, 1)
                    if c == 0:
                        pe.wait_ge(z_done, b * 4 + (2 * h + 2))
                        for f in range(KE):
                            last = nc.tensor.matmul(ps[:, TR + f, :], same_head[:, :], z[:, f, :],
                                                    start=True, stop=True)
                        last.then_inc(den_done, 1)
                    if c == 2:
                        pe.wait_ge(den_copied, b * 2 + (h + 1))
                        transpose_xn(split, next_ln)
                    for i in range(2):
                        pe.wait_ge(masked, b * 2 * N_CH + (2 * n + i + 1))
                        for g in (2 * i, 2 * i + 1):
                            for f in range(KE):
                                for v in range(2):
                                    last = nc.tensor.matmul(ps[32 * g:32 * g + 32, NUM, f * P:f * P + P],
                                                            v_padded(c, 8 * f + 2 * g + v),
                                                            scores[:, g, f, v, :], start=False, stop=True,
                                                            skip_group_check=True)
                    last.then_inc(pv_done, 1)

            def output(split, b, h):
                for i in range(2):
                    for t in (2 * i, 2 * i + 1):
                        tok = slice(t * P, t * P + P)
                        pe.wait_ge(o_lo_done if split else o_done, b * N_CH + (T * h + t + 1))
                        if split:
                            terms = [(oT16[:, f, s, tok], wo16[:, f, r, :]) for f in range(KE) for s, r in pairs]
                        else:
                            terms = [(oT[:, f, tok], wo[:, f, :]) for f in range(KE)]
                        last = product(ps[:, TR + i, (t % 2) * E:(t % 2) * E + E], terms)
                    last.then_inc(op_done, 1)

            pe.wait_ge(biases_loaded, 16 * 3)
            pe.wait_ge(setup_steps, 1)
            nc.tensor.matmul(ps[:, TR, 0:E], ones[0:1, 0:P], bv_row[:, :], start=True, stop=True)
            nc.tensor.matmul(ps[:, TR, E:2 * E], ones[0:1, 0:P], bo_row[:, :], start=True,
                             stop=True).then_inc(bias_rows_done, 1)

            def program(split):
                if split:
                    pe.wait_ge(wg16_ready, 1)
                transpose_xn(split, 1)
                with pe.Fori(0, B) as b:
                    ln = b * N_LN
                    wait_xt(split, ln + 1)
                    for s in range(NS):
                        if s == KF:
                            wait_xt(split, ln + 2)
                        gate_up(split, b, 0, s)
                        if s == 4:
                            transpose_xn(split, ln + 2)
                        if s >= LAG:
                            down(split, b, 0, s - LAG)
                    transpose_xn(split, ln + 3)
                    down(split, b, 0, NS - 2)
                    wait_xt(split, ln + 3)
                    if split:
                        pe.wait_ge(split_ready, 1)
                    q_or_k_after_ffn(split, b)
                    v_and_k(split, b, 0)
                    chunks(split, b, 0, ln + 4)
                    wait_xt(split, ln + 4)
                    q_or_k(split, 1, 0)
                    q_or_k(split, 1, 1)
                    output(split, b, 0)
                    q_or_k(split, 1, 2)
                    q_or_k(split, 1, 3)
                    pe.wait_ge(res2_done, b * 4 + 2)
                    v_and_k(split, b, 1)
                    chunks(split, b, 1, ln + 5)
                    wait_xt(split, ln + 5)
                    for s in range(NS):
                        if s == KF:
                            down(split, b, 1, s - LAG)
                            wait_xt(split, ln + 6)
                        gate_up(split, b, 1, s)
                        if s == 1:
                            output(split, b, 1)
                        if s == 5:
                            transpose_xn(split, ln + 6)
                        if s >= LAG and s != KF:
                            down(split, b, 1, s - LAG)
                    down(split, b, 1, NS - 2)
                    transpose_xn(split, ln + 7)
                    down(split, b, 1, NS - 1)

            either(pe, program)


_OUT = ((B, L, E), "float32")


def kernel(**inputs):
    import numpy as np
    import concourse.bacc as bacc
    from concourse.bass_utils import run_bass_kernel_spmd

    a = {k: np.asarray(v) for k, v in inputs.items()}
    bias = a["L0_attn_qkv_b"]
    arrays = {
        "x": a["L0_attn_x"],
        "w_gate": a["L0_ffn_w_gate"].T,
        "w_up": a["L0_ffn_w_up"].T,
        "w_down": a["L0_ffn_w_down"].T,
        "w_qkv": a["L0_attn_qkv_w"],
        "b_cols": bias[:2 * E].reshape(4, P).T,
        "b_v": bias[2 * E:].reshape(1, E),
        "w_out": a["L0_attn_out_w"],
        "b_out": a["L0_attn_out_b"].reshape(1, E),
    }
    arrays = {k: np.ascontiguousarray(v) for k, v in arrays.items()}
    nc = bacc.Bacc("TRN2", target_bir_lowering=False, num_devices=1)
    args = [nc.dram_tensor(k, v.shape, mybir.dt.from_np(v.dtype), kind="ExternalInput").ap()
            for k, v in arrays.items()]
    args.append(nc.dram_tensor("out", _OUT[0], mybir.dt.from_np(np.dtype(_OUT[1])), kind="ExternalOutput").ap())
    build(nc, *args)
    r = run_bass_kernel_spmd(nc, [arrays], core_ids=[0])
    return r.results[0]["out"]
```
